# Optimizing a Trainium2 kernel written in Bass

```python
import numpy as np
import jax
import jax.numpy as jnp

def _softmax(x, axis=-1):
    return jax.nn.softmax(x, axis=axis)
def _gelu(x):
    return jax.nn.gelu(x, approximate=True)
def _silu(x):
    return jax.nn.silu(x)
def _sigmoid(x):
    return jax.nn.sigmoid(x)
def _layernorm(x, axis=-1, eps=1e-5):
    m = jnp.mean(x, axis=axis, keepdims=True)
    v = jnp.var(x, axis=axis, keepdims=True)
    return (x - m) / jnp.sqrt(v + eps)
def _scatter_add(tgt, idx, src, axis=0):
    return tgt.at[idx].add(src)
def _segment_sum(src, seg, n):
    return jax.ops.segment_sum(src, seg, n)

kernel_name = 'mk_conv_seq_d1_conv_nchw512_7d1596'

def setup_inputs(seed: int = 0):
    np.random.seed(seed)
    _w = jnp.asarray
    def _rec_inputs():
        import jax
        import jax.numpy as jnp
        _gk = jax.random.key(seed)
        x = 7.22e-05 + 1 * jax.random.normal(jax.random.fold_in(_gk, 1), (16, 512, 32, 32), jnp.float32)
        return x
    x = _rec_inputs()
    def _L0_conv_setup():
        import jax, jax.numpy as jnp
        import numpy as np
        B, C, H, W = (16, 512, 32, 32)
        GROUPS = 32
        EPS = 1e-05

        def _group_norm(x, w, b):
            Bs, Cs, Hs, Ws = x.shape
            xg = x.reshape(Bs, GROUPS, Cs // GROUPS, Hs, Ws)
            mean = xg.mean(axis=(2, 3, 4), keepdims=True)
            var = xg.var(axis=(2, 3, 4), keepdims=True)
            xn = (xg - mean) * jax.lax.rsqrt(var + EPS)
            xn = xn.reshape(Bs, Cs, Hs, Ws)
            return xn * w[None, :, None, None] + b[None, :, None, None]
        key = jax.random.key(seed)
        ks = jax.random.split(key, 7)
        s = 1.0 / np.sqrt(C)
        return {'x': jax.random.normal(ks[0], (B, C, H, W), dtype=jnp.float32), 'gn_w': jnp.ones((C,), dtype=jnp.float32), 'gn_b': jnp.zeros((C,), dtype=jnp.float32), 'qkv_w': jax.random.normal(ks[1], (3 * C, C), dtype=jnp.float32) * s, 'qkv_b': jnp.zeros((3 * C,), dtype=jnp.float32), 'proj_w': jax.random.normal(ks[2], (C, C), dtype=jnp.float32) * s, 'proj_b': jnp.zeros((C,), dtype=jnp.float32)}
    _L0_conv_all = _L0_conv_setup()
    _L0_conv_in = {k: v for k, v in _L0_conv_all.items() if k in ('gn_w', 'gn_b', 'qkv_w', 'qkv_b', 'proj_w', 'proj_b', )}
    del _L0_conv_all

    return {
        "x": x,
        "L0_conv_gn_w": _L0_conv_in["gn_w"],
        "L0_conv_gn_b": _L0_conv_in["gn_b"],
        "L0_conv_qkv_w": _L0_conv_in["qkv_w"],
        "L0_conv_qkv_b": _L0_conv_in["qkv_b"],
        "L0_conv_proj_w": _L0_conv_in["proj_w"],
        "L0_conv_proj_b": _L0_conv_in["proj_b"],
    }

def reference(x, L0_conv_gn_w, L0_conv_gn_b, L0_conv_qkv_w, L0_conv_qkv_b, L0_conv_proj_w, L0_conv_proj_b):
    import jax
    import jax.numpy as jnp
    def _L0_conv_ref(x, gn_w, gn_b, qkv_w, qkv_b, proj_w, proj_b):
        import jax, jax.numpy as jnp
        import numpy as np
        B, C, H, W = (16, 512, 32, 32)
        GROUPS = 32
        EPS = 1e-05

        def _group_norm(x, w, b):
            Bs, Cs, Hs, Ws = x.shape
            xg = x.reshape(Bs, GROUPS, Cs // GROUPS, Hs, Ws)
            mean = xg.mean(axis=(2, 3, 4), keepdims=True)
            var = xg.var(axis=(2, 3, 4), keepdims=True)
            xn = (xg - mean) * jax.lax.rsqrt(var + EPS)
            xn = xn.reshape(Bs, Cs, Hs, Ws)
            return xn * w[None, :, None, None] + b[None, :, None, None]
        Bs, Cs, Hs, Ws = x.shape
        N = Hs * Ws
        h = _group_norm(x, gn_w, gn_b)
        qkv = jnp.einsum('bchw,oc->bohw', h, qkv_w) + qkv_b[None, :, None, None]
        q, k, v = jnp.split(qkv, 3, axis=1)
        q = q.reshape(Bs, Cs, N).transpose(0, 2, 1)
        k = k.reshape(Bs, Cs, N).transpose(0, 2, 1)
        v = v.reshape(Bs, Cs, N).transpose(0, 2, 1)
        scale = 1.0 / np.sqrt(Cs)
        attn = jax.nn.softmax(jnp.einsum('bnc,bmc->bnm', q, k) * scale, axis=-1)
        h = jnp.einsum('bnm,bmc->bnc', attn, v)
        h = h.transpose(0, 2, 1).reshape(Bs, Cs, Hs, Ws)
        h = jnp.einsum('bchw,oc->bohw', h, proj_w) + proj_b[None, :, None, None]
        return x + h

    def _gn(v, G=32, eps=1e-5):
        B_, C_, H_, W_ = v.shape
        g = v.reshape(B_, G, C_ // G, H_, W_)
        m = jnp.mean(g, axis=(2, 3, 4), keepdims=True)
        s = jnp.var(g, axis=(2, 3, 4), keepdims=True)
        return ((g - m) / jnp.sqrt(s + eps)).reshape(v.shape)

    def _ln_c(v, eps=1e-6):
        m = jnp.mean(v, axis=1, keepdims=True)
        s = jnp.var(v, axis=1, keepdims=True)
        return (v - m) / jnp.sqrt(s + eps)

    def _ln_t(v, eps=1e-5):
        m = jnp.mean(v, axis=-1, keepdims=True)
        s = jnp.var(v, axis=-1, keepdims=True)
        return (v - m) / jnp.sqrt(s + eps)

    def _to_tokens(v):
        B_, C_, H_, W_ = v.shape
        return v.reshape(B_, C_, H_ * W_).transpose(0, 2, 1)
    def _from_tokens(t, like):
        B_, C_, H_, W_ = like.shape
        return t.transpose(0, 2, 1).reshape(B_, C_, H_, W_)

    x = _L0_conv_ref(x, L0_conv_gn_w, L0_conv_gn_b, L0_conv_qkv_w, L0_conv_qkv_b, L0_conv_proj_w, L0_conv_proj_b)
    return x


_drawn_inputs = setup_inputs


def setup_inputs(seed=0):
    import zlib

    import numpy as np

    out = dict(_drawn_inputs(seed))
    spreads = {'L0_conv_gn_w': (1.0, 0.6),
     'L0_conv_gn_b': (0.0, 0.1),
     'L0_conv_qkv_b': (0.0, 0.1),
     'L0_conv_proj_b': (0.0, 0.1)}
    factors = {}
    for name, (base, spread) in spreads.items():
        noise = np.random.default_rng([zlib.crc32(name.encode()), seed]).standard_normal(out[name].shape)
        drawn = base * np.exp(spread * noise) if base else spread * noise
        out[name] = jnp.asarray(drawn.astype(out[name].dtype))
    for name, factor in factors.items():
        out[name] = (out[name] * factor).astype(out[name].dtype)
    return out
```

```python
from contextlib import ExitStack

import concourse.bass as bass
from concourse import mybir

P = 128
GROUPS = 32
EPS = 1e-5

ALU = mybir.AluOpType
ACT = mybir.ActivationFunctionType
F32 = mybir.dt.float32
F32R = mybir.dt.float32r
I32 = mybir.dt.int32
AX_X = mybir.AxisListType.X


def at(b, per_batch, k):
    return b * per_batch + k


def wait(eng, sem, value):
    if isinstance(value, int) and value <= 0:
        return
    eng.wait_ge(sem, value)


def group_norm_attention(nc, x, gn_w, gn_b, qkv_w, qkv_b, projT, proj_b, out):
    B, C, H, W = x.shape
    N = H * W
    CT = C // P
    NT = N // P
    CH = 512
    TPC = CH // P
    GS = C // GROUPS
    SCALE = float(C) ** -0.5
    assert C == CH and N == 2 * CH and CT == 4

    xv = x.rearrange("b (j p) h w -> b p j (h w)", p=P)
    ov = out.rearrange("b (j p) h w -> b p j (h w)", p=P)
    wv = qkv_w.rearrange("(k t p) c -> k p t c", k=3, p=P)

    G0, V, G1, O0, O1 = 0, CT, CT + NT, 2 * CT + NT, 3 * CT + NT
    ACCS = 4 * CT + NT
    SPLITS = 2 * CT + NT
    HALVES = 2 * NT
    STATS = 2 * CT + 6
    SUBS = 4
    NEWTON = 3
    COEFS = 4 * NEWTON + 3
    OUTS = 2 * CT

    with ExitStack() as ctx:
        def sb(name, shape, dt=F32):
            return ctx.enter_context(nc.sbuf_tensor(name, shape, dt))

        def sem(name):
            return ctx.enter_context(nc.semaphore(name))

        ps_s = ctx.enter_context(nc.psum_tensor("ps_s", [P, 2, 2, CH], F32))
        ps_t = ctx.enter_context(nc.psum_tensor("ps_t", [P, 2, TPC, P], F32))
        ps_a = ctx.enter_context(nc.psum_tensor("ps_a", [P, 2, CH], F32))

        m_hi, m_lo = sb("m_hi", [P, CT, C], F32R), sb("m_lo", [P, CT, C], F32R)
        pv_hi, pv_lo = sb("pv_hi", [P, CT, C], F32R), sb("pv_lo", [P, CT, C], F32R)
        h_hi, h_lo = sb("h_hi", [P, CT, N], F32R), sb("h_lo", [P, CT, N], F32R)
        xs = sb("xs", [P, CT, N])
        ident = sb("ident", [P, P])
        gavg = sb("gavg", [P, P])
        gnw, gnb = sb("gnw", [P, CT]), sb("gnb", [P, CT])
        bqkv = sb("bqkv", [P, 3 * CT])
        bq, bv = bqkv[:, 0:CT], bqkv[:, 2 * CT:3 * CT]
        bp = sb("bp", [P, CT])
        gbias, obias = sb("gbias", [P, CT]), sb("obias", [P, CT])
        bn = sb("bn", [P, CT, 2, 6])
        bn4 = bn[:, :, :, :].rearrange("p j a (s v) -> p j (a s) v", v=3)
        dmean, dsq, dvar = (sb(n, [P, CT, SUBS]) for n in ("dmean", "dsq", "dvar"))
        gmean, vhalf, rstd, newt, c15 = (sb(n, [P, CT]) for n in ("gmean", "vhalf", "rstd", "newt", "c15"))
        ha, hm, hb = (sb(n, [P, CT]) for n in ("ha", "hm", "hb"))
        mx = sb("mx", [P, 2, 2])
        nbias, rsum, rinv = (sb(n, [P, 2]) for n in ("nbias", "rsum", "rinv"))

        x_in = sem("x_in")
        small_in = sem("small_in")
        w_in = [sem(f"w_in{k}") for k in range(4)]
        consts = sem("consts")
        w_mm, w_hi, w_lo = sem("w_mm"), sem("w_hi"), sem("w_lo")
        vec_mm, vec_out = sem("vec_mm"), sem("vec_out")
        stat = sem("stat")
        grp_mm = sem("grp_mm")
        coef = sem("coef")
        h_full, h_hid, h_lod = sem("h_full"), sem("h_hid"), sem("h_lod")
        acc_mm = sem("acc_mm")
        acc_hi = sem("acc_hi")
        acc_free = sem("acc_free")
        s_mm = sem("s_mm")
        s_max = sem("s_max")
        s_bias = sem("s_bias")
        s_exp = sem("s_exp")
        s_rinv = sem("s_rinv")
        s_prob = sem("s_prob")
        t_mm = sem("t_mm")
        t_hi = sem("t_hi")
        t_free = sem("t_free")
        res_in = [sem(f"res_in{k}") for k in range(2)]
        stored = [sem(f"stored{k}") for k in range(2)]


        def channel_stats(dve, b, part):
            j, half = divmod(part, 2)
            if part == 0:
                dve.wait_ge(x_in, at(b, 16, 16))
            nc.vector.bn_stats(bn[:, j, half, :], xs[:, j, half * CH:(half + 1) * CH]).then_inc(stat, 1)

        def group_mean_mm(pe, b):
            pe.wait_ge(stat, at(b, STATS, 2 * CT))
            for s in range(SUBS):
                mm = nc.tensor.matmul(ps_t[:, 0, 0, 0:CT], gavg[:, :], bn4[:, :, s, 1], start=(s == 0),
                                      stop=(s == SUBS - 1))
            mm.then_inc(grp_mm, 1)

        def group_deviation(dve, b):
            k = 2 * CT
            dve.wait_ge(grp_mm, at(b, 2, 1))
            nc.vector.tensor_copy(gmean[:, :], ps_t[:, 0, 0, 0:CT]).then_inc(stat, 1)
            dve.wait_ge(stat, at(b, STATS, k + 1))
            nc.vector.tensor_tensor(dmean[:, :, :], bn4[:, :, :, 1],
                                    gmean[:, :].unsqueeze(2).broadcast_to([P, CT, SUBS]),
                                    ALU.subtract).then_inc(stat, 1)
            dve.wait_ge(stat, at(b, STATS, k + 2))
            nc.vector.tensor_tensor(dsq[:, :, :], dmean[:, :, :], dmean[:, :, :], ALU.mult).then_inc(stat, 1)
            dve.wait_ge(stat, at(b, STATS, k + 3))
            nc.vector.scalar_tensor_tensor(out=dvar[:, :, :], in0=bn4[:, :, :, 2], scalar=SUBS / N,
                                           in1=dsq[:, :, :], op0=ALU.mult, op1=ALU.add).then_inc(stat, 1)

        def group_var_mm(pe, b):
            pe.wait_ge(stat, at(b, STATS, 2 * CT + 4))
            for s in range(SUBS):
                mm = nc.tensor.matmul(ps_t[:, 0, 0, 0:CT], gavg[:, :], dvar[:, :, s], start=(s == 0),
                                      stop=(s == SUBS - 1))
            mm.then_inc(grp_mm, 1)

        def rsqrt_seed(dve, b):
            dve.wait_ge(grp_mm, at(b, 2, 2))
            nc.vector.tensor_scalar(vhalf[:, :], ps_t[:, 0, 0, 0:CT], EPS, 0.5, ALU.add, ALU.mult).then_inc(stat, 1)
            dve.wait_ge(stat, at(b, STATS, STATS - 1))
            nc.vector.tensor_scalar(rstd[:, :].bitcast(I32), vhalf[:, :].bitcast(I32), -0.5,
                                    float(0x5F3759DF - 0x400000), ALU.mult, ALU.add).then_inc(stat, 1)

        def norm_coefs(pool, b):
            pool.wait_ge(stat, at(b, STATS, STATS))
            k = 0
            for _ in range(NEWTON):
                nc.gpsimd.tensor_tensor(newt[:, :], rstd[:, :], rstd[:, :], ALU.mult).then_inc(coef, 1)
                pool.wait_ge(coef, at(b, COEFS, k + 1))
                nc.gpsimd.tensor_tensor(newt[:, :], newt[:, :], vhalf[:, :], ALU.mult).then_inc(coef, 1)
                pool.wait_ge(coef, at(b, COEFS, k + 2))
                nc.gpsimd.tensor_tensor(newt[:, :], c15[:, :], newt[:, :], ALU.subtract).then_inc(coef, 1)
                pool.wait_ge(coef, at(b, COEFS, k + 3))
                nc.gpsimd.tensor_tensor(rstd[:, :], rstd[:, :], newt[:, :], ALU.mult).then_inc(coef, 1)
                pool.wait_ge(coef, at(b, COEFS, k + 4))
                k += 4
            nc.gpsimd.tensor_tensor(ha[:, :], rstd[:, :], gnw[:, :], ALU.mult).then_inc(coef, 1)
            pool.wait_ge(coef, at(b, COEFS, k + 1))
            nc.gpsimd.tensor_tensor(hm[:, :], gmean[:, :], ha[:, :], ALU.mult).then_inc(coef, 1)
            pool.wait_ge(coef, at(b, COEFS, k + 2))
            nc.gpsimd.tensor_tensor(hb[:, :], gnb[:, :], hm[:, :], ALU.subtract).then_inc(coef, 1)

        def normalize(act, b, j):
            if j == 0:
                act.wait_ge(coef, at(b, COEFS, COEFS))
            nc.scalar.activation(xs[:, j, :], xs[:, j, :], ACT.Identity, bias=hb[:, j:j + 1],
                                 scale=ha[:, j:j + 1]).then_inc(h_full, 1)
            act.wait_ge(h_full, at(b, CT, j + 1))
            nc.scalar.activation(h_hi[:, j, :], xs[:, j, :], ACT.Copy).then_inc(h_hid, 1)

        def normalize_lo(dve, b, j):
            dve.wait_ge(h_hid, at(b, CT, j + 1))
            nc.vector.tensor_tensor(h_lo[:, j, :], xs[:, j, :], h_hi[:, j, :].bitcast(F32),
                                    ALU.subtract).then_inc(h_lod, 1)

        with ExitStack() as setup:
            wraw = setup.enter_context(nc.sbuf_tensor("wraw", [P, 4, CT, C], F32))
            WQ, WK, WV, WPT = range(4)
            banks = [ps_s[:, i // 2, i % 2, :] for i in range(4)] + [ps_a[:, i, :] for i in range(2)]
            bank_of = [banks[i % 6] for i in range(2 * CT)]
            gb_ps, ob_ps = ps_t[:, 1, 0, 0:CT], ps_t[:, 1, 1, 0:CT]

            with nc.Block() as block:
                @block.sync
                def _(sp):
                    sp.dma_start(xs[:, :, :], xv[0]).then_inc(x_in, 16)
                    for k in range(3):
                        sp.dma_start(wraw[:, k, :, :], wv[k]).then_inc(w_in[k], 16)
                    sp.dma_start(wraw[:, WPT, :, :], projT.rearrange("(t p) o -> p t o", p=P)).then_inc(w_in[WPT], 16)

                @block.gpsimd
                def _(pool):
                    for vec, src in ((gnw, gn_w), (gnb, gn_b), (bqkv, qkv_b), (bp, proj_b)):
                        pool.dma_start(vec[:, :], src).then_inc(small_in, 16)
                    nc.gpsimd.memset(ident[:, :], 0.0).then_inc(consts, 1)
                    nc.gpsimd.memset(gavg[:, :], 1.0 / (GS * SUBS)).then_inc(consts, 1)
                    pool.wait_ge(consts, 2)
                    nc.gpsimd.affine_select(out=ident[:, :], in_=ident[:, :], compare_op=ALU.not_equal, fill=1.0,
                                            base=0, pattern=[[-1, P]], channel_multiplier=1).then_inc(consts, 1)
                    g3 = gavg[:, :].rearrange("p (g s) -> p g s", s=GS)
                    nc.gpsimd.affine_select(out=g3, in_=g3, compare_op=ALU.is_ge, fill=0.0, base=0,
                                            pattern=[[-GS, P // GS], [0, GS]],
                                            channel_multiplier=1).then_inc(consts, 1)
                    nc.gpsimd.memset(c15[:, :], 1.5).then_inc(consts, 1)
                    pool.wait_ge(consts, 5)
                    nc.gpsimd.affine_select(out=g3, in_=g3, compare_op=ALU.is_ge, fill=0.0, base=GS - 1,
                                            pattern=[[GS, P // GS], [0, GS]],
                                            channel_multiplier=-1).then_inc(consts, 1)
                    pool.wait_ge(small_in, 4 * 16)
                    norm_coefs(pool, 0)

                @block.tensor
                def _(pe):
                    def weight_product(i):
                        j, (left, right) = i % CT, ((WQ, WK) if i < CT else (WV, WPT))
                        pe.wait_ge(w_in[left], 16)
                        pe.wait_ge(w_in[right], 16)
                        if i >= 6:
                            pe.wait_ge(w_lo, i - 5)
                        for t in range(CT):
                            mm = nc.tensor.matmul(bank_of[i], wraw[:, left, t, j * P:(j + 1) * P],
                                                  wraw[:, right, t, :], start=(t == 0), stop=(t == CT - 1))
                        mm.then_inc(w_mm, 1)

                    pe.wait_ge(consts, 6)
                    weight_product(0)
                    group_mean_mm(pe, 0)
                    weight_product(1)
                    group_var_mm(pe, 0)
                    for i in range(2, 2 * CT):
                        weight_product(i)
                    pe.wait_ge(small_in, 4 * 16)
                    for w, b_, ps in ((WK, bq, gb_ps), (WPT, bv, ob_ps)):
                        for j in range(CT):
                            for t in range(CT):
                                mm = nc.tensor.matmul(ps[:, j:j + 1], wraw[:, w, t, j * P:(j + 1) * P],
                                                      b_[:, t:t + 1], start=(t == 0), stop=(t == CT - 1))
                    mm.then_inc(vec_mm, 1)

                @block.scalar
                def _(act):
                    def split_hi(i):
                        act.wait_ge(w_mm, i + 1)
                        nc.scalar.activation((m_hi if i < CT else pv_hi)[:, i % CT, :], bank_of[i],
                                             ACT.Copy).then_inc(w_hi, 1)
                    split_hi(0)
                    split_hi(1)
                    for j in range(CT):
                        normalize(act, 0, j)
                        if j:
                            split_hi(j + 1)
                    for i in range(CT + 1, 2 * CT):
                        split_hi(i)

                @block.vector
                def _(dve):
                    def split_lo(i):
                        dve.wait_ge(w_hi, i + 1)
                        hi, lo = (m_hi, m_lo) if i < CT else (pv_hi, pv_lo)
                        nc.vector.tensor_tensor(lo[:, i % CT, :], bank_of[i], hi[:, i % CT, :].bitcast(F32),
                                                ALU.subtract).then_inc(w_lo, 1)
                    for part in range(2 * CT):
                        channel_stats(dve, 0, part)
                    group_deviation(dve, 0)
                    split_lo(0)
                    rsqrt_seed(dve, 0)
                    split_lo(1)
                    for j in range(CT):
                        normalize_lo(dve, 0, j)
                        if j:
                            split_lo(j + 1)
                    for i in range(CT + 1, 2 * CT):
                        split_lo(i)
                    dve.wait_ge(vec_mm, 1)
                    nc.vector.tensor_copy(gbias[:, :], gb_ps).then_inc(vec_out, 1)
                    nc.vector.tensor_tensor(obias[:, :], ob_ps, bp[:, :], ALU.add).then_inc(vec_out, 1)

        g_hi, g_lo = sb("g_hi", [P, CT, CH], F32R), sb("g_lo", [P, CT, CH], F32R)
        v_hi, v_lo = sb("v_hi", [P, NT, C], F32R), sb("v_lo", [P, NT, C], F32R)
        prob = sb("prob", [P, 2, N])
        pt_hi, pt_lo = (sb(n, [P, 2, NT, CH], F32R) for n in ("pt_hi", "pt_lo"))
        res = sb("res", [P, 2, CH])


        def pe_batch(pe, b, nxt):
            def acc_bank(use):
                wait(pe, acc_free, at(b, ACCS, use - 1))
                return ps_a[:, use % 2, :]

            def products(out_, lhs, rhs, steps):
                for t in range(steps):
                    (lh, ll), (rh, rl) = lhs(t), rhs(t)
                    nc.tensor.matmul(out_, lh, rh, start=(t == 0), stop=False)
                    nc.tensor.matmul(out_, lh, rl, start=False, stop=False)
                    mm = nc.tensor.matmul(out_, ll, rh, start=False, stop=(t == steps - 1))
                return mm

            def g_tile(chunk, j):
                o = acc_bank((G0, G1)[chunk] + j)
                js, ns = slice(j * P, (j + 1) * P), slice(chunk * CH, (chunk + 1) * CH)
                products(o, lambda t: (m_hi[:, t, js], m_lo[:, t, js]),
                         lambda t: (h_hi[:, t, ns], h_lo[:, t, ns]), CT).then_inc(acc_mm, 1)

            def v_tile(m):
                o = acc_bank(V + m)
                ms = slice(m * P, (m + 1) * P)
                products(o, lambda t: (h_hi[:, t, ms], h_lo[:, t, ms]),
                         lambda t: (pv_hi[:, t, :], pv_lo[:, t, :]), CT).then_inc(acc_mm, 1)

            def scores(n):
                wait(pe, s_exp, at(b, NT, n - 1))
                i = slice(n % TPC * P, (n % TPC + 1) * P)
                for half in range(2):
                    ms = slice(half * CH, (half + 1) * CH)
                    products(ps_s[:, n % 2, half, :], lambda t: (g_hi[:, t, i], g_lo[:, t, i]),
                             lambda t: (h_hi[:, t, ms], h_lo[:, t, ms]), CT).then_inc(s_mm, 1)

            def transposes(n):
                pe.wait_ge(s_prob, at(b, NT, n + 1))
                for half in range(2):
                    wait(pe, t_free, at(b, HALVES, 2 * n + half - 1))
                    for i in range(TPC):
                        m = half * TPC + i
                        tr = nc.tensor.transpose(ps_t[:, half, i, :], prob[:, n % 2, m * P:(m + 1) * P], ident[:, :])
                    tr.then_inc(t_mm, 1)

            def output(chunk, j):
                pe.wait_ge(t_free, at(b, HALVES, (chunk + 1) * NT))
                o = acc_bank((O0, O1)[chunk] + j)
                js = slice(j * P, (j + 1) * P)
                products(o, lambda m: (v_hi[:, m, js], v_lo[:, m, js]),
                         lambda m: (pt_hi[:, chunk, m, :], pt_lo[:, chunk, m, :]), NT).then_inc(acc_mm, 1)

            pe.wait_ge(h_lod, at(b, CT, CT))
            for j in range(CT):
                g_tile(0, j)
            for m in range(NT):
                v_tile(m)
            pe.wait_ge(acc_free, at(b, ACCS, G0 + CT))
            scores(0)
            scores(1)
            transposes(0)
            scores(2)
            transposes(1)
            scores(3)
            transposes(2)
            for j in range(CT):
                g_tile(1, j)
            transposes(3)
            output(0, 0)
            if nxt is not None:
                pe.wait_ge(t_free, at(b, HALVES, NT))
                group_mean_mm(pe, nxt)
            pe.wait_ge(acc_free, at(b, ACCS, G1 + CT))
            scores(4)
            if nxt is not None:
                group_var_mm(pe, nxt)
            scores(5)
            if nxt is not None:
                pe.wait_ge(stat, at(nxt, STATS, STATS - 1))
            transposes(4)
            output(0, 1)
            scores(6)
            transposes(5)
            scores(7)
            transposes(6)
            output(0, 2)
            transposes(7)
            output(0, 3)
            for j in range(CT):
                output(1, j)

        def act_batch(act, b, nxt):
            def g_hi_half(chunk, j):
                use = (G0, G1)[chunk] + j
                act.wait_ge(acc_mm, at(b, ACCS, use + 1))
                nc.scalar.activation(g_hi[:, j, :], ps_a[:, use % 2, :], ACT.Identity,
                                     bias=gbias[:, j:j + 1]).then_inc(acc_hi, 1)

            def v_hi_half(m):
                act.wait_ge(acc_mm, at(b, ACCS, V + m + 1))
                nc.scalar.activation(v_hi[:, m, :], ps_a[:, (V + m) % 2, :], ACT.Copy).then_inc(acc_hi, 1)

            def exponentials(n):
                act.wait_ge(s_bias, at(b, NT, n + 1))
                wait(act, t_mm, at(b, HALVES, 2 * (n - 1)))
                nc.scalar.activation(prob[:, n % 2, :], ps_s[:, n % 2, :, :].rearrange("p a n -> p (a n)"), ACT.Exp,
                                     bias=nbias[:, n % 2:n % 2 + 1], scale=SCALE,
                                     accum_out=rsum[:, n % 2:n % 2 + 1]).then_inc(s_exp, 1)

            def pt_hi_half(n):
                for half in range(2):
                    act.wait_ge(t_mm, at(b, HALVES, 2 * n + half + 1))
                    nc.scalar.activation(pt_hi[:, n // TPC, half * TPC:(half + 1) * TPC,
                                               n % TPC * P:(n % TPC + 1) * P],
                                         ps_t[:, half, :, :], ACT.Copy).then_inc(t_hi, 1)

            for j in range(CT):
                g_hi_half(0, j)
            for m in range(NT):
                v_hi_half(m)
            exponentials(0)
            exponentials(1)
            pt_hi_half(0)
            exponentials(2)
            pt_hi_half(1)
            exponentials(3)
            pt_hi_half(2)
            for j in range(CT):
                g_hi_half(1, j)
            pt_hi_half(3)
            exponentials(4)
            exponentials(5)
            pt_hi_half(4)
            exponentials(6)
            pt_hi_half(5)
            exponentials(7)
            pt_hi_half(6)
            if nxt is not None:
                act.wait_ge(s_mm, at(b, HALVES, HALVES))
                normalize(act, nxt, 0)
            pt_hi_half(7)
            if nxt is not None:
                for j in range(1, CT):
                    normalize(act, nxt, j)

        def dve_batch(dve, b, nxt):
            def g_lo_half(chunk, j):
                use = (G0, G1)[chunk] + j
                dve.wait_ge(acc_hi, at(b, SPLITS, use + 1))
                nc.vector.scalar_tensor_tensor(out=g_lo[:, j, :], in0=ps_a[:, use % 2, :], scalar=gbias[:, j:j + 1],
                                               in1=g_hi[:, j, :].bitcast(F32), op0=ALU.add,
                                               op1=ALU.subtract).then_inc(acc_free, 1)

            def v_lo_half(m):
                dve.wait_ge(acc_hi, at(b, SPLITS, V + m + 1))
                nc.vector.tensor_tensor(v_lo[:, m, :], ps_a[:, (V + m) % 2, :], v_hi[:, m, :].bitcast(F32),
                                        ALU.subtract).then_inc(acc_free, 1)

            def row_max(n):
                for half in range(2):
                    dve.wait_ge(s_mm, at(b, HALVES, 2 * n + half + 1))
                    nc.vector.reduce_max(mx[:, n % 2, half:half + 1], ps_s[:, n % 2, half, :], AX_X)\
                        .then_inc(s_max, 1)
                dve.wait_ge(s_max, at(b, HALVES, 2 * n + 2))
                nc.vector.tensor_scalar(nbias[:, n % 2:n % 2 + 1], mx[:, n % 2, 0:1], mx[:, n % 2, 1:2], -SCALE,
                                        ALU.max, ALU.mult).then_inc(s_bias, 1)

            def probabilities(n):
                dve.wait_ge(s_exp, at(b, NT, n + 1))
                nc.vector.reciprocal(rinv[:, n % 2:n % 2 + 1], rsum[:, n % 2:n % 2 + 1]).then_inc(s_rinv, 1)
                dve.wait_ge(s_rinv, at(b, NT, n + 1))
                nc.vector.tensor_scalar(prob[:, n % 2, :], prob[:, n % 2, :], rinv[:, n % 2:n % 2 + 1], None,
                                        ALU.mult).then_inc(s_prob, 1)

            def pt_lo_half(n):
                for half in range(2):
                    dve.wait_ge(t_hi, at(b, HALVES, 2 * n + half + 1))
                    to = (slice(None), n // TPC, slice(half * TPC, (half + 1) * TPC),
                          slice(n % TPC * P, (n % TPC + 1) * P))
                    nc.vector.tensor_tensor(pt_lo[to], ps_t[:, half, :, :], pt_hi[to].bitcast(F32),
                                            ALU.subtract).then_inc(t_free, 1)

            def finish(chunk, j):
                k = chunk * CT + j
                use = O0 + k
                dve.wait_ge(acc_mm, at(b, ACCS, use + 1))
                dve.wait_ge(res_in[k % 2], at(b, 8 * OUTS, 16 * (k // 2 + 1)))
                nc.vector.scalar_tensor_tensor(out=res[:, k % 2, :], in0=ps_a[:, use % 2, :],
                                               scalar=obias[:, j:j + 1], in1=res[:, k % 2, :], op0=ALU.add,
                                               op1=ALU.add).then_inc(acc_free, 1)

            for j in range(CT):
                g_lo_half(0, j)
            for m in range(NT):
                v_lo_half(m)
                if nxt is not None:
                    channel_stats(dve, nxt, m)
            row_max(0)
            probabilities(0)
            row_max(1)
            pt_lo_half(0)
            probabilities(1)
            row_max(2)
            pt_lo_half(1)
            probabilities(2)
            row_max(3)
            pt_lo_half(2)
            probabilities(3)
            for j in range(CT):
                g_lo_half(1, j)
            pt_lo_half(3)
            finish(0, 0)
            if nxt is not None:
                group_deviation(dve, nxt)
            row_max(4)
            probabilities(4)
            if nxt is not None:
                rsqrt_seed(dve, nxt)
            row_max(5)
            pt_lo_half(4)
            probabilities(5)
            finish(0, 1)
            row_max(6)
            pt_lo_half(5)
            probabilities(6)
            row_max(7)
            pt_lo_half(6)
            probabilities(7)
            finish(0, 2)
            if nxt is not None:
                normalize_lo(dve, nxt, 0)
            pt_lo_half(7)
            if nxt is not None:
                normalize_lo(dve, nxt, 1)
            finish(0, 3)
            if nxt is not None:
                normalize_lo(dve, nxt, 2)
            finish(1, 0)
            if nxt is not None:
                normalize_lo(dve, nxt, 3)
            for j in range(1, CT):
                finish(1, j)

        def tile_of(view, b, k):
            ns = slice(k // CT * CH, (k // CT + 1) * CH)
            if isinstance(b, int):
                return view[b, :, k % CT, ns]
            return view[bass.ds(b, 1), :, k % CT, ns].rearrange("b p n -> (b p) n")

        def sp_batch(sp, b, nxt):
            if nxt is not None:
                sp.wait_ge(h_lod, at(b, CT, CT))
                src = xv[nxt] if isinstance(nxt, int) else \
                    xv[bass.ds(nxt, 1), :, :, :].rearrange("b p j n -> (b p) j n")
                sp.dma_start(xs[:, :, :], src).then_inc(x_in, 16)
            for k in range(OUTS):
                sp.wait_ge(acc_free, at(b, ACCS, O0 + k + 1))
                sp.dma_start(tile_of(ov, b, k), res[:, k % 2, :]).then_inc(stored[k % 2], 16)
                if k + 2 < OUTS or nxt is not None:
                    sp.wait_ge(stored[k % 2], at(b, 8 * OUTS, 16 * (k // 2 + 1)))
                    nb, nk = (b, k + 2) if k + 2 < OUTS else (nxt, k + 2 - OUTS)
                    sp.dma_start(res[:, k % 2, :], tile_of(xv, nb, nk)).then_inc(res_in[k % 2], 16)

        with nc.Block() as block:
            def batches(eng, body):
                body(eng, 0, 1)
                with eng.Fori(1, B - 1) as b:
                    body(eng, b, b + 1)
                body(eng, B - 1, None)

            @block.sync
            def _(sp):
                for k in range(2):
                    sp.dma_start(res[:, k, :], tile_of(xv, 0, k)).then_inc(res_in[k], 16)
                batches(sp, sp_batch)
                for k in range(2):
                    sp.wait_ge(stored[k], at(B, 8 * OUTS, 0))

            @block.gpsimd
            def _(pool):
                with pool.Fori(1, B) as b:
                    norm_coefs(pool, b)

            @block.tensor
            def _(pe):
                batches(pe, pe_batch)

            @block.scalar
            def _(act):
                batches(act, act_batch)

            @block.vector
            def _(dve):
                batches(dve, dve_batch)


def kernel(x, L0_conv_gn_w, L0_conv_gn_b, L0_conv_qkv_w, L0_conv_qkv_b, L0_conv_proj_w, L0_conv_proj_b):
    import numpy as np
    import concourse.bacc as bacc
    from concourse.bass_utils import run_bass_kernel_spmd

    def columns(v):
        return np.asarray(v).reshape(-1, P).T

    nc = bacc.Bacc("TRN2", target_bir_lowering=False, num_devices=1)
    host = {
        "x": x, "gn_w": columns(L0_conv_gn_w), "gn_b": columns(L0_conv_gn_b), "qkv_w": L0_conv_qkv_w,
        "qkv_b": columns(L0_conv_qkv_b), "projT": np.asarray(L0_conv_proj_w).T, "proj_b": columns(L0_conv_proj_b),
    }
    arrays = {f"in_{k}": np.ascontiguousarray(a) for k, a in host.items()}
    args = [nc.dram_tensor(k, a.shape, mybir.dt.from_np(a.dtype), kind="ExternalInput").ap()
            for k, a in arrays.items()]
    out = nc.dram_tensor("out", arrays["in_x"].shape, mybir.dt.float32, kind="ExternalOutput").ap()
    group_norm_attention(nc, *args, out)
    r = run_bass_kernel_spmd(nc, [arrays], core_ids=[0])
    return r.results[0]["out"]
```

```python
from contextlib import ExitStack

import concourse.bass as bass
from concourse import mybir

P = 128
GROUPS = 32
EPS = 1e-5

ALU = mybir.AluOpType
ACT = mybir.ActivationFunctionType
F32 = mybir.dt.float32
F32R = mybir.dt.float32r
I32 = mybir.dt.int32
RMAX = bass.bass_isa.ReduceOp.max
RADD = bass.bass_isa.ReduceOp.add


def at(b, per_batch, k):
    return b * per_batch + k


def wait(eng, sem, value):
    if isinstance(value, int) and value <= 0:
        return
    eng.wait_ge(sem, value)


def group_norm_attention(nc, x, gn_w, gn_b, qkv_w, qkv_b, projT, proj_b, out):
    B, C, H, W = x.shape
    N = H * W
    CT = C // P
    NT = N // P
    CH = 512
    GS = C // GROUPS
    SCALE = float(C) ** -0.5
    BANKS = 8
    assert C == CH and N == 2 * CH and CT == 4

    xv = x.rearrange("b (j p) h w -> b p j (h w)", p=P)
    ov = out.rearrange("b (j p) h w -> b p j (h w)", p=P)
    wv = qkv_w.rearrange("(k t p) c -> k p t c", k=3, p=P)
    wpv = projT.rearrange("(t p) o -> p t o", p=P)

    G0 = 0
    V0 = G0 + CT
    S0 = V0 + 1
    VM = S0 + NT
    G1 = VM + NT - 2
    VL = G1 + CT
    S1 = VL + 1
    O0 = S1 + NT
    O1 = O0 + CT
    USES = O1 + CT
    assert USES % BANKS == 0
    SPLIT_USES = [*range(G0, V0), V0, *range(VM, G1), *range(G1, VL), VL]
    RAW_USES = [*range(S0, VM), *range(S1, O0)]
    OUT_USES = [*range(O0, USES)]
    SPLITS, RAWS, OUTS = len(SPLIT_USES), len(RAW_USES), len(OUT_USES)

    def v_use(m):
        return V0 if m == 0 else VL if m == NT - 1 else VM + m - 1

    MAXES = 2 * (NT - 1)
    STATS = 2 * CT + 6
    SUBS = 4
    NEWTON = 3
    COEFS = 4 * NEWTON + 3
    STAT_BANK = (S1 + NT - 1) % BANKS

    with ExitStack() as ctx:
        def sb(name, shape, dt=F32):
            return ctx.enter_context(nc.sbuf_tensor(name, shape, dt))

        def sem(name):
            return ctx.enter_context(nc.semaphore(name))

        ps = ctx.enter_context(nc.psum_tensor("ps", [P, BANKS, CH], F32))

        m_hi, m_lo = sb("m_hi", [P, CT, C], F32R), sb("m_lo", [P, CT, C], F32R)
        pv_hi, pv_lo = sb("pv_hi", [P, CT, C], F32R), sb("pv_lo", [P, CT, C], F32R)
        h_hi, h_lo = sb("h_hi", [P, CT, N], F32R), sb("h_lo", [P, CT, N], F32R)
        xs = sb("xs", [P, CT, N])
        res = sb("res", [P, 2, CT, CH])
        gavg = sb("gavg", [P, P])
        gnw, gnb = sb("gnw", [P, CT]), sb("gnb", [P, CT])
        bqkv = sb("bqkv", [P, 3 * CT])
        bq, bv = bqkv[:, 0:CT], bqkv[:, 2 * CT:3 * CT]
        bp = sb("bp", [P, CT])
        gbias, obias = sb("gbias", [P, CT]), sb("obias", [P, CT])
        bn = sb("bn", [P, CT, 2, 6])
        bn4 = bn[:, :, :, :].rearrange("p j a (s v) -> p j (a s) v", v=3)
        dmean, dsq, dvar = (sb(n, [P, CT, SUBS]) for n in ("dmean", "dsq", "dvar"))
        gmean, vhalf, rstd, newt, c15 = (sb(n, [P, CT]) for n in ("gmean", "vhalf", "rstd", "newt", "c15"))
        ha, hm, hb = (sb(n, [P, CT]) for n in ("ha", "hm", "hb"))
        rmax, cmax, esum = (sb(n, [P, CH]) for n in ("rmax", "cmax", "esum"))
        rinv = sb("rinv", [P, 2, CH])

        WQ, WK, WV, WPT = range(4)
        with ExitStack() as early:
            wraw = early.enter_context(nc.sbuf_tensor("wraw", [P, 4, CT, C], F32))
            ws_hi = early.enter_context(nc.sbuf_tensor("ws_hi", [P, 4, CT, C], F32R))
            ws_lo = early.enter_context(nc.sbuf_tensor("ws_lo", [P, 4, CT, C], F32R))
        g_hi, g_lo = sb("g_hi", [P, CT, CH], F32R), sb("g_lo", [P, CT, CH], F32R)
        v_hi, v_lo = sb("v_hi", [P, NT, C], F32R), sb("v_lo", [P, NT, C], F32R)
        st = sb("st", [P, NT, CH])
        pt_hi, pt_lo = sb("pt_hi", [P, NT, CH], F32R), sb("pt_lo", [P, NT, CH], F32R)

        x_in = sem("x_in")
        small_in = sem("small_in")
        w_in = [[sem(f"w_in{k}{t}") for t in range(CT)] for k in range(4)]
        consts = sem("consts")
        ws_hid, ws_lod = sem("ws_hid"), sem("ws_lod")
        wp_mm, wp_hid, wp_lod = sem("wp_mm"), sem("wp_hid"), sem("wp_lod")
        vec_mm, vec_out = sem("vec_mm"), sem("vec_out")
        stat = sem("stat")
        grp_mm = sem("grp_mm")
        coef = sem("coef")
        h_full, h_hid, h_lod = sem("h_full"), sem("h_hid"), sem("h_lod")
        split_mm = sem("split_mm")
        split_hi = sem("split_hi")
        split_lo = sem("split_lo")
        raw_mm = sem("raw_mm")
        raw_out = sem("raw_out")
        maxed = sem("maxed")
        max_all = sem("max_all")
        shifted = sem("shifted")
        exped = sem("exped")
        pt_hid = sem("pt_hid")
        pt_lod = sem("pt_lod")
        summed = sem("summed")
        sum_all = sem("sum_all")
        inverse = sem("inverse")
        out_mm = sem("out_mm")
        scaled = sem("scaled")
        finished = sem("finished")
        res_in = [sem(f"res_in{k}") for k in range(2)]
        stored = [sem(f"stored{k}") for k in range(2)]
        pool_at = sem("pool_at")


        def channel_stats(dve, b, part):
            j, half = divmod(part, 2)
            if part == 0:
                dve.wait_ge(x_in, at(b, 16, 16))
            nc.vector.bn_stats(bn[:, j, half, :], xs[:, j, half * CH:(half + 1) * CH]).then_inc(stat, 1)

        def group_mean_mm(pe, b, bank):
            pe.wait_ge(stat, at(b, STATS, 2 * CT))
            for s in range(SUBS):
                mm = nc.tensor.matmul(ps[:, bank, 0:CT], gavg[:, :], bn4[:, :, s, 1], start=(s == 0),
                                      stop=(s == SUBS - 1))
            mm.then_inc(grp_mm, 1)

        def group_deviation(dve, b, bank):
            k = 2 * CT
            dve.wait_ge(grp_mm, at(b, 2, 1))
            nc.vector.tensor_copy(gmean[:, :], ps[:, bank, 0:CT]).then_inc(stat, 1)
            dve.wait_ge(stat, at(b, STATS, k + 1))
            nc.vector.tensor_tensor(dmean[:, :, :], bn4[:, :, :, 1],
                                    gmean[:, :].unsqueeze(2).broadcast_to([P, CT, SUBS]),
                                    ALU.subtract).then_inc(stat, 1)
            dve.wait_ge(stat, at(b, STATS, k + 2))
            nc.vector.tensor_tensor(dsq[:, :, :], dmean[:, :, :], dmean[:, :, :], ALU.mult).then_inc(stat, 1)
            dve.wait_ge(stat, at(b, STATS, k + 3))
            nc.vector.scalar_tensor_tensor(out=dvar[:, :, :], in0=bn4[:, :, :, 2], scalar=SUBS / N,
                                           in1=dsq[:, :, :], op0=ALU.mult, op1=ALU.add).then_inc(stat, 1)

        def group_var_mm(pe, b, bank):
            pe.wait_ge(stat, at(b, STATS, 2 * CT + 4))
            for s in range(SUBS):
                mm = nc.tensor.matmul(ps[:, bank, 0:CT], gavg[:, :], dvar[:, :, s], start=(s == 0),
                                      stop=(s == SUBS - 1))
            mm.then_inc(grp_mm, 1)

        def rsqrt_seed(dve, b, bank):
            dve.wait_ge(grp_mm, at(b, 2, 2))
            nc.vector.tensor_scalar(vhalf[:, :], ps[:, bank, 0:CT], EPS, 0.5, ALU.add, ALU.mult).then_inc(stat, 1)
            dve.wait_ge(stat, at(b, STATS, STATS - 1))
            nc.vector.tensor_scalar(rstd[:, :].bitcast(I32), vhalf[:, :].bitcast(I32), -0.5,
                                    float(0x5F3759DF - 0x400000), ALU.mult, ALU.add).then_inc(stat, 1)

        def norm_coefs(pool, b):
            pool.wait_ge(stat, at(b, STATS, STATS))
            k = 0
            for _ in range(NEWTON):
                nc.gpsimd.tensor_tensor(newt[:, :], rstd[:, :], rstd[:, :], ALU.mult).then_inc(coef, 1)
                pool.wait_ge(coef, at(b, COEFS, k + 1))
                nc.gpsimd.tensor_tensor(newt[:, :], newt[:, :], vhalf[:, :], ALU.mult).then_inc(coef, 1)
                pool.wait_ge(coef, at(b, COEFS, k + 2))
                nc.gpsimd.tensor_tensor(newt[:, :], c15[:, :], newt[:, :], ALU.subtract).then_inc(coef, 1)
                pool.wait_ge(coef, at(b, COEFS, k + 3))
                nc.gpsimd.tensor_tensor(rstd[:, :], rstd[:, :], newt[:, :], ALU.mult).then_inc(coef, 1)
                pool.wait_ge(coef, at(b, COEFS, k + 4))
                k += 4
            nc.gpsimd.tensor_tensor(ha[:, :], rstd[:, :], gnw[:, :], ALU.mult).then_inc(coef, 1)
            pool.wait_ge(coef, at(b, COEFS, k + 1))
            nc.gpsimd.tensor_tensor(hm[:, :], gmean[:, :], ha[:, :], ALU.mult).then_inc(coef, 1)
            pool.wait_ge(coef, at(b, COEFS, k + 2))
            nc.gpsimd.tensor_tensor(hb[:, :], gnb[:, :], hm[:, :], ALU.subtract).then_inc(coef, 1)

        def normalize(act, b, j):
            if j == 0:
                act.wait_ge(coef, at(b, COEFS, COEFS))
            nc.scalar.activation(xs[:, j, :], xs[:, j, :], ACT.Identity, bias=hb[:, j:j + 1],
                                 scale=ha[:, j:j + 1]).then_inc(h_full, 1)
            act.wait_ge(h_full, at(b, CT, j + 1))
            nc.scalar.activation(h_hi[:, j, :], xs[:, j, :], ACT.Copy).then_inc(h_hid, 1)

        def normalize_lo(dve, b, j):
            dve.wait_ge(h_hid, at(b, CT, j + 1))
            nc.vector.tensor_tensor(h_lo[:, j, :], xs[:, j, :], h_hi[:, j, :].bitcast(F32),
                                    ALU.subtract).then_inc(h_lod, 1)

        def product(bank, lhs, rhs, first, last):
            (lh, ll), (rh, rl) = lhs, rhs
            nc.tensor.matmul(ps[:, bank, :], lh, rh, start=first, stop=False)
            nc.tensor.matmul(ps[:, bank, :], lh, rl, start=False, stop=False)
            return nc.tensor.matmul(ps[:, bank, :], ll, rh, start=False, stop=last)

        PAIRS = ((WQ, WK), (WV, WPT))

        def load_weights(sp, pair):
            for t in range(CT):
                for k in PAIRS[pair]:
                    src = wpv[:, t, :] if k == WPT else wv[k, :, t, :]
                    sp.dma_start(wraw[:, k, t, :], src).then_inc(w_in[k][t], 16)

        def weight_product(pe, pair):
            left, right = PAIRS[pair]
            for t in range(CT):
                pe.wait_ge(ws_lod, pair * 2 * CT + 2 * t + 2)
                for j in range(CT):
                    js = slice(j * P, (j + 1) * P)
                    mm = product(pair * CT + j, (ws_hi[:, left, t, js], ws_lo[:, left, t, js]),
                                 (ws_hi[:, right, t, :], ws_lo[:, right, t, :]), t == 0, t == CT - 1)
                    if t == CT - 1:
                        mm.then_inc(wp_mm, 1)

        def weight_hi(act, pair, t):
            for k in PAIRS[pair]:
                act.wait_ge(w_in[k][t], 16)
                nc.scalar.activation(ws_hi[:, k, t, :], wraw[:, k, t, :], ACT.Copy).then_inc(ws_hid, 1)

        def weight_lo(dve, pair, t):
            for i, k in enumerate(PAIRS[pair]):
                dve.wait_ge(ws_hid, (pair * CT + t) * 2 + i + 1)
                nc.vector.tensor_tensor(ws_lo[:, k, t, :], wraw[:, k, t, :], ws_hi[:, k, t, :].bitcast(F32),
                                        ALU.subtract).then_inc(ws_lod, 1)

        def weight_product_hi(act, pair, j):
            act.wait_ge(wp_mm, pair * CT + j + 1)
            nc.scalar.activation((m_hi, pv_hi)[pair][:, j, :], ps[:, pair * CT + j, :], ACT.Copy).then_inc(wp_hid, 1)

        def weight_product_lo(dve, pair, j):
            dve.wait_ge(wp_hid, pair * CT + j + 1)
            nc.vector.tensor_tensor((m_lo, pv_lo)[pair][:, j, :], ps[:, pair * CT + j, :],
                                    (m_hi, pv_hi)[pair][:, j, :].bitcast(F32), ALU.subtract).then_inc(wp_lod, 1)

        def sp_setup(sp):
            load_weights(sp, 0)
            sp.dma_start(xs[:, :, :], xv[0]).then_inc(x_in, 16)
            load_weights(sp, 1)
            for ch in range(2):
                sp.dma_start(res[:, ch, :, :], xv[0, :, :, ch * CH:(ch + 1) * CH]).then_inc(res_in[ch], 16)
            sp.wait_ge(h_lod, CT)
            sp.dma_start(xs[:, :, :], xv[1]).then_inc(x_in, 16)

        def pool_setup(pool):
            for vec, src in ((gnw, gn_w), (gnb, gn_b), (bqkv, qkv_b), (bp, proj_b)):
                pool.dma_start(vec[:, :], src).then_inc(small_in, 16)
            nc.gpsimd.memset(c15[:, :], 1.5).then_inc(consts, 1)
            nc.gpsimd.memset(gavg[:, :], 1.0 / (GS * SUBS)).then_inc(consts, 1)
            pool.wait_ge(consts, 2)
            g3 = gavg[:, :].rearrange("p (g s) -> p g s", s=GS)
            nc.gpsimd.affine_select(out=g3, in_=g3, compare_op=ALU.is_ge, fill=0.0, base=0,
                                    pattern=[[-GS, P // GS], [0, GS]], channel_multiplier=1).then_inc(consts, 1)
            pool.wait_ge(consts, 3)
            nc.gpsimd.affine_select(out=g3, in_=g3, compare_op=ALU.is_ge, fill=0.0, base=GS - 1,
                                    pattern=[[GS, P // GS], [0, GS]], channel_multiplier=-1).then_inc(consts, 1)
            pool.wait_ge(small_in, 4 * 16)
            norm_coefs(pool, 0)

        def pe_setup(pe):
            weight_product(pe, 0)
            pe.wait_ge(consts, 4)
            pe.wait_ge(wp_lod, 1)
            group_mean_mm(pe, 0, 0)
            pe.wait_ge(small_in, 4 * 16)
            pe.wait_ge(wp_lod, 2)
            for j in range(CT):
                for t in range(CT):
                    nc.tensor.matmul(ps[:, 1, j:j + 1], wraw[:, WK, t, j * P:(j + 1) * P], bq[:, t:t + 1],
                                     start=(t == 0), stop=(t == CT - 1))
            group_var_mm(pe, 0, 0)
            weight_product(pe, 1)
            for j in range(CT):
                for t in range(CT):
                    mm = nc.tensor.matmul(ps[:, 1, CT + j:CT + j + 1], wraw[:, WPT, t, j * P:(j + 1) * P],
                                          bv[:, t:t + 1], start=(t == 0), stop=(t == CT - 1))
            mm.then_inc(vec_mm, 1)
            pe.wait_ge(wp_lod, 2 * CT)
            pe.wait_ge(vec_out, 2)

        def act_setup(act):
            for t in range(CT):
                weight_hi(act, 0, t)
            for j in range(CT):
                weight_product_hi(act, 0, j)
            for t in range(CT):
                weight_hi(act, 1, t)
            for j in range(CT):
                normalize(act, 0, j)
            for j in range(CT):
                weight_product_hi(act, 1, j)

        def dve_setup(dve):
            for t in range(CT):
                weight_lo(dve, 0, t)
            for part in range(2 * CT):
                channel_stats(dve, 0, part)
            for j in range(CT):
                weight_product_lo(dve, 0, j)
            group_deviation(dve, 0, 0)
            weight_lo(dve, 1, 0)
            rsqrt_seed(dve, 0, 0)
            for t in range(1, CT):
                weight_lo(dve, 1, t)
            for j in range(CT):
                normalize_lo(dve, 0, j)
            for j in range(CT):
                weight_product_lo(dve, 1, j)
            dve.wait_ge(vec_mm, 1)
            nc.vector.tensor_copy(gbias[:, :], ps[:, 1, 0:CT]).then_inc(vec_out, 1)
            nc.vector.tensor_tensor(obias[:, :], ps[:, 1, CT:2 * CT], bp[:, :], ALU.add).then_inc(vec_out, 1)


        def pe_batch(pe, b, nxt):
            def bank(use):
                before = (use - BANKS) % USES
                ago = 0 if use >= BANKS else 1
                if before in SPLIT_USES:
                    wait(pe, split_lo, at(b, SPLITS, SPLIT_USES.index(before) + 1 - ago * SPLITS))
                elif before in RAW_USES:
                    wait(pe, raw_out, at(b, RAWS, RAW_USES.index(before) + 1 - ago * RAWS))
                else:
                    wait(pe, finished, at(b, OUTS, OUT_USES.index(before) + 1 - ago * OUTS))
                return use % BANKS

            def g_tile(chunk, j):
                o = bank((G0, G1)[chunk] + j)
                js, ns = slice(j * P, (j + 1) * P), slice(chunk * CH, (chunk + 1) * CH)
                for t in range(CT):
                    mm = product(o, (m_hi[:, t, js], m_lo[:, t, js]), (h_hi[:, t, ns], h_lo[:, t, ns]),
                                 t == 0, t == CT - 1)
                mm.then_inc(split_mm, 1)

            def v_tile(m):
                o = bank(v_use(m))
                ms = slice(m * P, (m + 1) * P)
                for t in range(CT):
                    mm = product(o, (h_hi[:, t, ms], h_lo[:, t, ms]), (pv_hi[:, t, :], pv_lo[:, t, :]),
                                 t == 0, t == CT - 1)
                mm.then_inc(split_mm, 1)

            def scores(chunk, m):
                if m == 0:
                    pe.wait_ge(split_lo, at(b, SPLITS, SPLIT_USES.index((G0, G1)[chunk] + CT - 1) + 1))
                o = bank((S0, S1)[chunk] + m)
                ms = slice(m * P, (m + 1) * P)
                for t in range(CT):
                    mm = product(o, (h_hi[:, t, ms], h_lo[:, t, ms]), (g_hi[:, t, :], g_lo[:, t, :]),
                                 t == 0, t == CT - 1)
                mm.then_inc(raw_mm, 1)

            def outputs(chunk):
                for m in range(NT):
                    pe.wait_ge(pt_lod, at(b, RAWS, chunk * NT + m + 1))
                    for j in range(CT):
                        use = (O0, O1)[chunk] + j
                        o = bank(use) if m == 0 else use % BANKS
                        js = slice(j * P, (j + 1) * P)
                        mm = product(o, (v_hi[:, m, js], v_lo[:, m, js]), (pt_hi[:, m, :], pt_lo[:, m, :]),
                                     m == 0, m == NT - 1)
                    mm.then_inc(out_mm, 1)

            pe.wait_ge(h_lod, at(b, CT, CT))
            for j in range(CT):
                g_tile(0, j)
            v_tile(0)
            for m in range(NT):
                scores(0, m)
            for m in range(1, NT - 1):
                v_tile(m)
            for j in range(CT):
                g_tile(1, j)
            v_tile(NT - 1)
            for m in range(NT):
                if nxt is not None and m == NT - 4:
                    pe.wait_ge(split_lo, at(b, SPLITS, SPLIT_USES.index(S1 + NT - 1 - BANKS) + 1))
                    group_mean_mm(pe, nxt, STAT_BANK)
                if nxt is not None and m == NT - 2:
                    group_var_mm(pe, nxt, STAT_BANK)
                if nxt is not None and m == NT - 1:
                    pe.wait_ge(stat, at(nxt, STATS, STATS - 1))
                scores(1, m)
            outputs(0)
            outputs(1)

        def act_batch(act, b, nxt):
            def g_hi_half(chunk, j):
                use = (G0, G1)[chunk] + j
                act.wait_ge(split_mm, at(b, SPLITS, SPLIT_USES.index(use) + 1))
                nc.scalar.activation(g_hi[:, j, :], ps[:, use % BANKS, :], ACT.Identity,
                                     bias=gbias[:, j:j + 1]).then_inc(split_hi, 1)

            def v_hi_half(m):
                use = v_use(m)
                act.wait_ge(split_mm, at(b, SPLITS, SPLIT_USES.index(use) + 1))
                nc.scalar.activation(v_hi[:, m, :], ps[:, use % BANKS, :], ACT.Copy).then_inc(split_hi, 1)

            def raw_scores(chunk, m):
                k = chunk * NT + m
                act.wait_ge(raw_mm, at(b, RAWS, k + 1))
                wait(act, pt_lod, at(b, RAWS, k + 1 - NT))
                wait(act, summed, at(b, MAXES, (chunk - 1) * (NT - 1) + max(m, 1)))
                nc.scalar.activation(st[:, m, :], ps[:, RAW_USES[k] % BANKS, :], ACT.Copy).then_inc(raw_out, 1)

            def exponentials(chunk, m):
                act.wait_ge(shifted, at(b, RAWS, chunk * NT + m + 1))
                nc.scalar.activation(st[:, m, :], st[:, m, :], ACT.Exp, scale=SCALE).then_inc(exped, 1)

            def pt_hi_half(chunk, m):
                k = chunk * NT + m
                act.wait_ge(exped, at(b, RAWS, k + 1))
                wait(act, out_mm, at(b, RAWS, k + 1 - NT))
                nc.scalar.activation(pt_hi[:, m, :], st[:, m, :], ACT.Copy).then_inc(pt_hid, 1)

            for j in range(CT):
                g_hi_half(0, j)
            v_hi_half(0)
            for m in range(NT):
                raw_scores(0, m)
            v_hi_half(1)
            v_hi_half(2)
            for m in range(NT):
                exponentials(0, m)
                pt_hi_half(0, m)
                if m < NT - 4:
                    v_hi_half(m + 3)
                else:
                    g_hi_half(1, m - (NT - 4))
            v_hi_half(NT - 1)
            for m in range(NT):
                raw_scores(1, m)
            if nxt is not None:
                normalize(act, nxt, 0)
            for m in range(NT):
                exponentials(1, m)
                pt_hi_half(1, m)
                if nxt is not None and m in (1, 3, 5):
                    normalize(act, nxt, (m + 1) // 2)

        def dve_batch(dve, b, nxt):
            def g_lo_half(chunk, j):
                use = (G0, G1)[chunk] + j
                dve.wait_ge(split_hi, at(b, SPLITS, SPLIT_USES.index(use) + 1))
                nc.vector.scalar_tensor_tensor(out=g_lo[:, j, :], in0=ps[:, use % BANKS, :],
                                               scalar=gbias[:, j:j + 1], in1=g_hi[:, j, :].bitcast(F32),
                                               op0=ALU.add, op1=ALU.subtract).then_inc(split_lo, 1)

            def v_lo_half(m):
                use = v_use(m)
                dve.wait_ge(split_hi, at(b, SPLITS, SPLIT_USES.index(use) + 1))
                nc.vector.tensor_tensor(v_lo[:, m, :], ps[:, use % BANKS, :], v_hi[:, m, :].bitcast(F32),
                                        ALU.subtract).then_inc(split_lo, 1)

            def running_max(chunk, m):
                k = chunk * (NT - 1) + m
                dve.wait_ge(raw_out, at(b, RAWS, chunk * NT + m + 1))
                if m == 1:
                    wait(dve, max_all, at(b, 2, chunk))
                else:
                    dve.wait_ge(maxed, at(b, MAXES, k - 1))
                nc.vector.tensor_tensor(rmax[:, :], st[:, 0, :] if m == 1 else rmax[:, :], st[:, m, :],
                                        ALU.max).then_inc(maxed, 1)

            def shift(chunk, m):
                dve.wait_ge(max_all, at(b, 2, chunk + 1))
                nc.vector.tensor_tensor(st[:, m, :], st[:, m, :], cmax[:, :], ALU.subtract).then_inc(shifted, 1)

            def pt_lo_half(chunk, m):
                dve.wait_ge(pt_hid, at(b, RAWS, chunk * NT + m + 1))
                nc.vector.tensor_tensor(pt_lo[:, m, :], st[:, m, :], pt_hi[:, m, :].bitcast(F32),
                                        ALU.subtract).then_inc(pt_lod, 1)

            def finish(chunk):
                dve.wait_ge(sum_all, at(b, 2, chunk + 1))
                nc.vector.reciprocal(rinv[:, chunk, :], rinv[:, chunk, :]).then_inc(inverse, 1)
                dve.wait_ge(inverse, at(b, 2, chunk + 1))
                for j in range(CT):
                    o = ((O0, O1)[chunk] + j) % BANKS
                    dve.wait_ge(out_mm, at(b, RAWS, (chunk + 1) * NT))
                    nc.vector.tensor_tensor(ps[:, o, :], ps[:, o, :], rinv[:, chunk, :], ALU.mult).then_inc(scaled, 1)
                for j in range(CT):
                    o = ((O0, O1)[chunk] + j) % BANKS
                    dve.wait_ge(res_in[chunk], at(b, 16, 16))
                    dve.wait_ge(scaled, at(b, OUTS, chunk * CT + j + 1))
                    nc.vector.scalar_tensor_tensor(out=res[:, chunk, j, :], in0=ps[:, o, :],
                                                   scalar=obias[:, j:j + 1], in1=res[:, chunk, j, :],
                                                   op0=ALU.add, op1=ALU.add).then_inc(finished, 1)

            for j in range(CT):
                g_lo_half(0, j)
            v_lo_half(0)
            for m in range(NT):
                if m:
                    running_max(0, m)
                if nxt is not None:
                    channel_stats(dve, nxt, m)
            v_lo_half(1)
            v_lo_half(2)
            shift(0, 0)
            for m in range(NT):
                if m < NT - 1:
                    shift(0, m + 1)
                pt_lo_half(0, m)
                if m < NT - 4:
                    v_lo_half(m + 3)
                else:
                    g_lo_half(1, m - (NT - 4))
            v_lo_half(NT - 1)
            for m in range(1, NT):
                running_max(1, m)
                if nxt is not None and m == NT - 4:
                    group_deviation(dve, nxt, STAT_BANK)
                if nxt is not None and m == NT - 2:
                    rsqrt_seed(dve, nxt, STAT_BANK)
            shift(1, 0)
            for m in range(NT):
                if m < NT - 1:
                    shift(1, m + 1)
                pt_lo_half(1, m)
                if nxt is not None and m in (1, 3, 5, 7):
                    normalize_lo(dve, nxt, m // 2)
            finish(0)
            finish(1)

        def pool_batch(pool, b, nxt):
            def max_over_partitions(chunk):
                pool.wait_ge(maxed, at(b, MAXES, (chunk + 1) * (NT - 1)))
                wait(pool, shifted, at(b, RAWS, chunk * NT))
                pool.sem_inc(pool_at, 1)
                nc.gpsimd.partition_all_reduce(cmax[:, :], rmax[:, :], P, RMAX).then_inc(max_all, 1)

            def running_sum(chunk, m):
                k = chunk * (NT - 1) + m
                pool.wait_ge(exped, at(b, RAWS, chunk * NT + m + 1))
                if m == 1:
                    wait(pool, sum_all, at(b, 2, chunk))
                else:
                    pool.wait_ge(summed, at(b, MAXES, k - 1))
                nc.gpsimd.tensor_tensor(esum[:, :], st[:, 0, :] if m == 1 else esum[:, :], st[:, m, :],
                                        ALU.add).then_inc(summed, 1)

            def sum_over_partitions(chunk):
                wait(pool, finished, at(b, OUTS, (chunk + 1) * CT - OUTS))
                pool.wait_ge(summed, at(b, MAXES, (chunk + 1) * (NT - 1)))
                pool.sem_inc(pool_at, 1)
                nc.gpsimd.partition_all_reduce(rinv[:, chunk, :], esum[:, :], P, RADD).then_inc(sum_all, 1)

            max_over_partitions(0)
            for m in range(1, NT):
                running_sum(0, m)
            sum_over_partitions(0)
            if nxt is not None:
                norm_coefs(pool, nxt)
            max_over_partitions(1)
            for m in range(1, NT):
                running_sum(1, m)
            sum_over_partitions(1)

        def chunk_of(view, b, ch):
            ns = slice(ch * CH, (ch + 1) * CH)
            if isinstance(b, int):
                return view[b, :, :, ns]
            return view[bass.ds(b, 1), :, :, ns].rearrange("b p j n -> (b p) j n")

        def sp_batch(sp, b, nxt, after):
            for ch in range(2):
                sp.wait_ge(finished, at(b, OUTS, (ch + 1) * CT))
                sp.dma_start(chunk_of(ov, b, ch), res[:, ch, :, :]).then_inc(stored[ch], 16)
                if nxt is not None:
                    sp.wait_ge(stored[ch], at(b, 16, 16))
                    sp.dma_start(res[:, ch, :, :], chunk_of(xv, nxt, ch)).then_inc(res_in[ch], 16)
                if ch == 0 and after is not None:
                    sp.wait_ge(h_lod, at(nxt, CT, CT))
                    src = xv[after] if isinstance(after, int) else \
                        xv[bass.ds(after, 1), :, :, :].rearrange("b p j n -> (b p) j n")
                    sp.dma_start(xs[:, :, :], src).then_inc(x_in, 16)

        block = ctx.enter_context(nc.Block())

        def batches(eng, body):
            body(eng, 0, 1)
            with eng.Fori(1, B - 1) as b:
                body(eng, b, b + 1)
            body(eng, B - 1, None)

        @block.sync
        def _(sp):
            sp_setup(sp)
            sp_batch(sp, 0, 1, 2)
            with sp.Fori(1, B - 2) as b:
                sp_batch(sp, b, b + 1, b + 2)
            sp_batch(sp, B - 2, B - 1, None)
            sp_batch(sp, B - 1, None, None)
            for ch in range(2):
                sp.wait_ge(stored[ch], B * 16)

        @block.gpsimd
        def _(pool):
            pool_setup(pool)
            batches(pool, pool_batch)

        @block.tensor
        def _(pe):
            pe_setup(pe)
            batches(pe, pe_batch)

        @block.scalar
        def _(act):
            act_setup(act)
            batches(act, act_batch)

        @block.vector
        def _(dve):
            dve_setup(dve)
            batches(dve, dve_batch)


def kernel(x, L0_conv_gn_w, L0_conv_gn_b, L0_conv_qkv_w, L0_conv_qkv_b, L0_conv_proj_w, L0_conv_proj_b):
    import numpy as np
    import concourse.bacc as bacc
    from concourse.bass_utils import run_bass_kernel_spmd

    def columns(v):
        return np.asarray(v).reshape(-1, P).T

    nc = bacc.Bacc("TRN2", target_bir_lowering=False, num_devices=1)
    host = {
        "x": x, "gn_w": columns(L0_conv_gn_w), "gn_b": columns(L0_conv_gn_b), "qkv_w": L0_conv_qkv_w,
        "qkv_b": columns(L0_conv_qkv_b), "projT": np.asarray(L0_conv_proj_w).T, "proj_b": columns(L0_conv_proj_b),
    }
    arrays = {f"in_{k}": np.ascontiguousarray(a) for k, a in host.items()}
    args = [nc.dram_tensor(k, a.shape, mybir.dt.from_np(a.dtype), kind="ExternalInput").ap()
            for k, a in arrays.items()]
    out = nc.dram_tensor("out", arrays["in_x"].shape, mybir.dt.float32, kind="ExternalOutput").ap()
    group_norm_attention(nc, *args, out)
    r = run_bass_kernel_spmd(nc, [arrays], core_ids=[0])
    return r.results[0]["out"]
```

```python
from contextlib import ExitStack

import concourse.bass as bass
from concourse import mybir

P = 128
GROUPS = 32
EPS = 1e-5

ALU = mybir.AluOpType
ACT = mybir.ActivationFunctionType
F32 = mybir.dt.float32
F32R = mybir.dt.float32r
I32 = mybir.dt.int32
AX_X = mybir.AxisListType.X
RMAX = bass.bass_isa.ReduceOp.max
RADD = bass.bass_isa.ReduceOp.add


def at(b, per_batch, k):
    return b * per_batch + k


def wait(eng, sem, value):
    if isinstance(value, int) and value <= 0:
        return
    eng.wait_ge(sem, value)


def group_norm_attention(nc, x, gn_w, gn_b, qkv_w, qkv_b, projT, proj_b, out):
    B, C, H, W = x.shape
    N = H * W
    CT = C // P
    NT = N // P
    CH = 512
    GS = C // GROUPS
    SCALE = float(C) ** -0.5
    BANKS = 8
    assert C == CH and N == 2 * CH and CT == 4

    xv = x.rearrange("b (j p) h w -> b p j (h w)", p=P)
    ov = out.rearrange("b (j p) h w -> b p j (h w)", p=P)
    wv = qkv_w.rearrange("(k t p) c -> k p t c", k=3, p=P)
    wpv = projT.rearrange("(t p) o -> p t o", p=P)

    G0 = 0
    V0 = G0 + CT
    S0 = V0 + 1
    VM = S0 + NT
    G1 = VM + NT - 2
    VL = G1 + CT
    S1 = VL + 1
    O0 = S1 + NT
    O1 = O0 + CT
    USES = O1 + CT
    assert USES % BANKS == 0
    SPLIT_USES = [*range(G0, V0), V0, *range(VM, G1), *range(G1, VL), VL]
    RAW_USES = [*range(S0, VM), *range(S1, O0)]
    OUT_USES = [*range(O0, USES)]
    SPLITS, RAWS, OUTS = len(SPLIT_USES), len(RAW_USES), len(OUT_USES)

    def v_use(m):
        return V0 if m == 0 else VL if m == NT - 1 else VM + m - 1

    MAXES = 2 * (NT - 1)
    STATS = 2 * CT + 8
    SUBS = 4
    NEWTON = 3
    COEFS = 4 * NEWTON + 3
    STAT_BANK = (S1 + NT - 1) % BANKS

    with ExitStack() as ctx:
        def sb(name, shape, dt=F32):
            return ctx.enter_context(nc.sbuf_tensor(name, shape, dt))

        def sem(name):
            return ctx.enter_context(nc.semaphore(name))

        ps = ctx.enter_context(nc.psum_tensor("ps", [P, BANKS, CH], F32))

        m_hi, m_lo = sb("m_hi", [P, CT, C], F32R), sb("m_lo", [P, CT, C], F32R)
        pv_hi, pv_lo = sb("pv_hi", [P, CT, C], F32R), sb("pv_lo", [P, CT, C], F32R)
        h_hi, h_lo = sb("h_hi", [P, CT, N], F32R), sb("h_lo", [P, CT, N], F32R)
        xs = sb("xs", [P, CT, N])
        res = sb("res", [P, 2, CT, CH])
        gavg = sb("gavg", [P, P])
        gnw, gnb = sb("gnw", [P, CT]), sb("gnb", [P, CT])
        bqkv = sb("bqkv", [P, 3 * CT])
        bq, bv = bqkv[:, 0:CT], bqkv[:, 2 * CT:3 * CT]
        bp = sb("bp", [P, CT])
        gbias, obias = sb("gbias", [P, CT]), sb("obias", [P, CT])
        bn = sb("bn", [P, CT, 2, 6])
        bn4 = bn[:, :, :, :].rearrange("p j a (s v) -> p j (a s) v", v=3)
        msum, vsum = sb("msum", [P, CT]), sb("vsum", [P, CT])
        dmean, dsq, dvar = (sb(n, [P, CT, SUBS]) for n in ("dmean", "dsq", "dvar"))
        gmean, vhalf, rstd, newt, c15 = (sb(n, [P, CT]) for n in ("gmean", "vhalf", "rstd", "newt", "c15"))
        ha, hm, hb = (sb(n, [P, CT]) for n in ("ha", "hm", "hb"))
        rmax, cmax, esum = (sb(n, [P, CH]) for n in ("rmax", "cmax", "esum"))
        rinv = sb("rinv", [P, 2, CH])

        WQ, WK, WV, WPT = range(4)
        with ExitStack() as early:
            wraw = early.enter_context(nc.sbuf_tensor("wraw", [P, 4, CT, C], F32))
            ws_hi = early.enter_context(nc.sbuf_tensor("ws_hi", [P, 4, CT, C], F32R))
            ws_lo = early.enter_context(nc.sbuf_tensor("ws_lo", [P, 4, CT, C], F32R))
        g_hi, g_lo = sb("g_hi", [P, CT, CH], F32R), sb("g_lo", [P, CT, CH], F32R)
        v_hi, v_lo = sb("v_hi", [P, NT, C], F32R), sb("v_lo", [P, NT, C], F32R)
        st = sb("st", [P, NT, CH])
        pt_hi, pt_lo = sb("pt_hi", [P, NT, CH], F32R), sb("pt_lo", [P, NT, CH], F32R)

        x_in = sem("x_in")
        small_in = sem("small_in")
        w_in = [[sem(f"w_in{k}{t}") for t in range(CT)] for k in range(4)]
        consts = sem("consts")
        ws_hid = sem("ws_hid")
        ws_lod, ws_lod_pool = sem("ws_lod"), sem("ws_lod_pool")
        wp_mm, wp_hid, wp_lod = sem("wp_mm"), sem("wp_hid"), sem("wp_lod")
        vec_mm, vec_out = sem("vec_mm"), sem("vec_out")
        stat = sem("stat")
        grp_mm = sem("grp_mm")
        coef = sem("coef")
        h_full, h_hid, h_lod = sem("h_full"), sem("h_hid"), sem("h_lod")
        split_mm = sem("split_mm")
        split_hi = sem("split_hi")
        split_lo = sem("split_lo")
        raw_mm = sem("raw_mm")
        raw_out = sem("raw_out")
        maxed = sem("maxed")
        max_all = sem("max_all")
        shifted = sem("shifted")
        exped = sem("exped")
        pt_hid = sem("pt_hid")
        pt_lod = sem("pt_lod")
        summed = sem("summed")
        sum_all = sem("sum_all")
        inverse = sem("inverse")
        out_mm = sem("out_mm")
        scaled = sem("scaled")
        finished = sem("finished")
        res_in = [sem(f"res_in{k}") for k in range(2)]
        stored = [sem(f"stored{k}") for k in range(2)]
        pool_at = sem("pool_at")


        def channel_stats(dve, b, part):
            j, half = divmod(part, 2)
            if part == 0:
                dve.wait_ge(x_in, at(b, 16, 16))
            nc.vector.bn_stats(bn[:, j, half, :], xs[:, j, half * CH:(half + 1) * CH]).then_inc(stat, 1)

        def channel_means(dve, b):
            dve.wait_ge(stat, at(b, STATS, 2 * CT))
            nc.vector.reduce_sum(msum[:, :], bn4[:, :, :, 1], AX_X).then_inc(stat, 1)

        def group_mean_mm(pe, b, bank):
            pe.wait_ge(stat, at(b, STATS, 2 * CT + 1))
            nc.tensor.matmul(ps[:, bank, 0:CT], gavg[:, :], msum[:, :], start=True, stop=True).then_inc(grp_mm, 1)

        def group_deviation(dve, b, bank):
            k = 2 * CT + 1
            dve.wait_ge(grp_mm, at(b, 2, 1))
            nc.vector.tensor_copy(gmean[:, :], ps[:, bank, 0:CT]).then_inc(stat, 1)
            dve.wait_ge(stat, at(b, STATS, k + 1))
            nc.vector.tensor_tensor(dmean[:, :, :], bn4[:, :, :, 1],
                                    gmean[:, :].unsqueeze(2).broadcast_to([P, CT, SUBS]),
                                    ALU.subtract).then_inc(stat, 1)
            dve.wait_ge(stat, at(b, STATS, k + 2))
            nc.vector.tensor_tensor(dsq[:, :, :], dmean[:, :, :], dmean[:, :, :], ALU.mult).then_inc(stat, 1)
            dve.wait_ge(stat, at(b, STATS, k + 3))
            nc.vector.scalar_tensor_tensor(out=dvar[:, :, :], in0=bn4[:, :, :, 2], scalar=SUBS / N,
                                           in1=dsq[:, :, :], op0=ALU.mult, op1=ALU.add).then_inc(stat, 1)
            dve.wait_ge(stat, at(b, STATS, k + 4))
            nc.vector.reduce_sum(vsum[:, :], dvar[:, :, :], AX_X).then_inc(stat, 1)

        def group_var_mm(pe, b, bank):
            pe.wait_ge(stat, at(b, STATS, 2 * CT + 6))
            nc.tensor.matmul(ps[:, bank, 0:CT], gavg[:, :], vsum[:, :], start=True, stop=True).then_inc(grp_mm, 1)

        def rsqrt_seed(dve, b, bank):
            dve.wait_ge(grp_mm, at(b, 2, 2))
            nc.vector.tensor_scalar(vhalf[:, :], ps[:, bank, 0:CT], EPS, 0.5, ALU.add, ALU.mult).then_inc(stat, 1)
            dve.wait_ge(stat, at(b, STATS, STATS - 1))
            nc.vector.tensor_scalar(rstd[:, :].bitcast(I32), vhalf[:, :].bitcast(I32), -0.5,
                                    float(0x5F3759DF - 0x400000), ALU.mult, ALU.add).then_inc(stat, 1)

        def norm_coefs(pool, b):
            pool.wait_ge(stat, at(b, STATS, STATS))
            k = 0
            for _ in range(NEWTON):
                nc.gpsimd.tensor_tensor(newt[:, :], rstd[:, :], rstd[:, :], ALU.mult).then_inc(coef, 1)
                pool.wait_ge(coef, at(b, COEFS, k + 1))
                nc.gpsimd.tensor_tensor(newt[:, :], newt[:, :], vhalf[:, :], ALU.mult).then_inc(coef, 1)
                pool.wait_ge(coef, at(b, COEFS, k + 2))
                nc.gpsimd.tensor_tensor(newt[:, :], c15[:, :], newt[:, :], ALU.subtract).then_inc(coef, 1)
                pool.wait_ge(coef, at(b, COEFS, k + 3))
                nc.gpsimd.tensor_tensor(rstd[:, :], rstd[:, :], newt[:, :], ALU.mult).then_inc(coef, 1)
                pool.wait_ge(coef, at(b, COEFS, k + 4))
                k += 4
            nc.gpsimd.tensor_tensor(ha[:, :], rstd[:, :], gnw[:, :], ALU.mult).then_inc(coef, 1)
            pool.wait_ge(coef, at(b, COEFS, k + 1))
            nc.gpsimd.tensor_tensor(hm[:, :], gmean[:, :], ha[:, :], ALU.mult).then_inc(coef, 1)
            pool.wait_ge(coef, at(b, COEFS, k + 2))
            nc.gpsimd.tensor_tensor(hb[:, :], gnb[:, :], hm[:, :], ALU.subtract).then_inc(coef, 1)

        def normalize(act, b, j):
            if j == 0:
                act.wait_ge(coef, at(b, COEFS, COEFS))
            nc.scalar.activation(xs[:, j, :], xs[:, j, :], ACT.Identity, bias=hb[:, j:j + 1],
                                 scale=ha[:, j:j + 1]).then_inc(h_full, 1)
            act.wait_ge(h_full, at(b, CT, j + 1))
            nc.scalar.activation(h_hi[:, j, :], xs[:, j, :], ACT.Copy).then_inc(h_hid, 1)

        def normalize_lo(dve, b, j):
            dve.wait_ge(h_hid, at(b, CT, j + 1))
            nc.vector.tensor_tensor(h_lo[:, j, :], xs[:, j, :], h_hi[:, j, :].bitcast(F32),
                                    ALU.subtract).then_inc(h_lod, 1)

        def product(bank, lhs, rhs, first, last):
            (lh, ll), (rh, rl) = lhs, rhs
            nc.tensor.matmul(ps[:, bank, :], lh, rh, start=first, stop=False)
            nc.tensor.matmul(ps[:, bank, :], lh, rl, start=False, stop=False)
            return nc.tensor.matmul(ps[:, bank, :], ll, rh, start=False, stop=last)

        PAIRS = ((WQ, WK), (WV, WPT))
        U_BANK, O_BANK, NORM_BANK = 6, 0, 7
        POOL_TILES = 2

        def load_weights(sp, pair):
            for t in range(CT):
                for k in PAIRS[pair]:
                    src = wpv[:, t, :] if k == WPT else wv[k, :, t, :]
                    sp.dma_start(wraw[:, k, t, :], src).then_inc(w_in[k][t], 16)

        def weight_product(pe, pair):
            left, right = PAIRS[pair]
            for t in range(CT):
                if pair == 0:
                    pe.wait_ge(ws_lod, 2 * t + 2)
                elif t < POOL_TILES:
                    pe.wait_ge(ws_lod_pool, 2 * t + 2)
                else:
                    pe.wait_ge(ws_lod, 2 * (CT - POOL_TILES + t) + 2)
                for j in range(CT):
                    if pair == 1 and t == 0 and j == U_BANK - CT:
                        pe.wait_ge(vec_out, 1)
                    if pair == 1 and t == 0 and j == NORM_BANK - CT:
                        pe.wait_ge(stat, STATS - 1)
                    js = slice(j * P, (j + 1) * P)
                    mm = product(pair * CT + j, (ws_hi[:, left, t, js], ws_lo[:, left, t, js]),
                                 (ws_hi[:, right, t, :], ws_lo[:, right, t, :]), t == 0, t == CT - 1)
                    if t == CT - 1:
                        mm.then_inc(wp_mm, 1)

        def weight_hi(act, pair, t):
            for k in PAIRS[pair]:
                act.wait_ge(w_in[k][t], 16)
                nc.scalar.activation(ws_hi[:, k, t, :], wraw[:, k, t, :], ACT.Copy).then_inc(ws_hid, 1)

        def weight_lo(eng, lod, pair, t):
            for i, k in enumerate(PAIRS[pair]):
                eng.wait_ge(ws_hid, (pair * CT + t) * 2 + i + 1)
                eng.tensor_tensor(ws_lo[:, k, t, :], wraw[:, k, t, :], ws_hi[:, k, t, :].bitcast(F32),
                                  ALU.subtract).then_inc(lod, 1)

        def weight_product_hi(act, pair, j):
            act.wait_ge(wp_mm, pair * CT + j + 1)
            nc.scalar.activation((m_hi, pv_hi)[pair][:, j, :], ps[:, pair * CT + j, :], ACT.Copy).then_inc(wp_hid, 1)

        def weight_product_lo(dve, pair, j):
            dve.wait_ge(wp_hid, pair * CT + j + 1)
            nc.vector.tensor_tensor((m_lo, pv_lo)[pair][:, j, :], ps[:, pair * CT + j, :],
                                    (m_hi, pv_hi)[pair][:, j, :].bitcast(F32), ALU.subtract).then_inc(wp_lod, 1)

        def sp_setup(sp):
            load_weights(sp, 0)
            sp.dma_start(xs[:, :, :], xv[0]).then_inc(x_in, 16)
            load_weights(sp, 1)
            for ch in range(2):
                sp.dma_start(res[:, ch, :, :], xv[0, :, :, ch * CH:(ch + 1) * CH]).then_inc(res_in[ch], 16)
            sp.wait_ge(h_lod, CT)
            sp.dma_start(xs[:, :, :], xv[1]).then_inc(x_in, 16)

        def pool_setup(pool):
            for vec, src in ((gnw, gn_w), (gnb, gn_b), (bqkv, qkv_b), (bp, proj_b)):
                pool.dma_start(vec[:, :], src).then_inc(small_in, 16)
            nc.gpsimd.memset(c15[:, :], 1.5).then_inc(consts, 1)
            nc.gpsimd.memset(gavg[:, :], 1.0 / (GS * SUBS)).then_inc(consts, 1)
            pool.wait_ge(consts, 2)
            g3 = gavg[:, :].rearrange("p (g s) -> p g s", s=GS)
            nc.gpsimd.affine_select(out=g3, in_=g3, compare_op=ALU.is_ge, fill=0.0, base=0,
                                    pattern=[[-GS, P // GS], [0, GS]], channel_multiplier=1).then_inc(consts, 1)
            pool.wait_ge(consts, 3)
            nc.gpsimd.affine_select(out=g3, in_=g3, compare_op=ALU.is_ge, fill=0.0, base=GS - 1,
                                    pattern=[[GS, P // GS], [0, GS]], channel_multiplier=-1).then_inc(consts, 1)
            pool.wait_ge(small_in, 4 * 16)
            for t in range(POOL_TILES):
                weight_lo(pool, ws_lod_pool, 1, t)
            norm_coefs(pool, 0)

        def pe_setup(pe):
            weight_product(pe, 0)
            pe.wait_ge(small_in, 4 * 16)
            vector_product(pe, WK, bq, U_BANK)
            pe.wait_ge(consts, 4)
            group_mean_mm(pe, 0, NORM_BANK)
            group_var_mm(pe, 0, NORM_BANK)
            weight_product(pe, 1)
            pe.wait_ge(wp_lod, 1)
            vector_product(pe, WPT, bv, O_BANK)

        def vector_product(pe, w, vec, bank):
            for j in range(CT):
                for t in range(CT):
                    mm = nc.tensor.matmul(ps[:, bank, j:j + 1], wraw[:, w, t, j * P:(j + 1) * P],
                                          vec[:, t:t + 1], start=(t == 0), stop=(t == CT - 1))
            mm.then_inc(vec_mm, 1)

        def act_setup(act):
            for t in range(CT):
                weight_hi(act, 0, t)
            weight_hi(act, 1, 0)
            weight_hi(act, 1, 1)
            for j in range(CT):
                weight_product_hi(act, 0, j)
            weight_hi(act, 1, 2)
            weight_hi(act, 1, 3)
            for j in range(CT):
                normalize(act, 0, j)
            for j in range(CT):
                weight_product_hi(act, 1, j)

        def dve_setup(dve):
            for t in range(CT):
                weight_lo(dve, ws_lod, 0, t)
            for part in range(2 * CT):
                channel_stats(dve, 0, part)
            channel_means(dve, 0)
            dve.wait_ge(vec_mm, 1)
            nc.vector.tensor_copy(gbias[:, :], ps[:, U_BANK, 0:CT]).then_inc(vec_out, 1)
            group_deviation(dve, 0, NORM_BANK)
            rsqrt_seed(dve, 0, NORM_BANK)
            weight_product_lo(dve, 0, 0)
            for t in range(POOL_TILES, CT):
                weight_lo(dve, ws_lod, 1, t)
            for j in range(1, CT):
                weight_product_lo(dve, 0, j)
            for j in range(CT):
                normalize_lo(dve, 0, j)
            for j in range(CT):
                weight_product_lo(dve, 1, j)
            dve.wait_ge(vec_mm, 2)
            nc.vector.tensor_tensor(obias[:, :], ps[:, O_BANK, 0:CT], bp[:, :], ALU.add).then_inc(vec_out, 1)


        def pe_batch(pe, b, nxt):
            def bank(use):
                before = (use - BANKS) % USES
                ago = 0 if use >= BANKS else 1
                if before in SPLIT_USES:
                    wait(pe, split_lo, at(b, SPLITS, SPLIT_USES.index(before) + 1 - ago * SPLITS))
                elif before in RAW_USES:
                    wait(pe, raw_out, at(b, RAWS, RAW_USES.index(before) + 1 - ago * RAWS))
                else:
                    wait(pe, finished, at(b, OUTS, OUT_USES.index(before) + 1 - ago * OUTS))
                return use % BANKS

            def g_tile(chunk, j):
                o = bank((G0, G1)[chunk] + j)
                js, ns = slice(j * P, (j + 1) * P), slice(chunk * CH, (chunk + 1) * CH)
                for t in range(CT):
                    mm = product(o, (m_hi[:, t, js], m_lo[:, t, js]), (h_hi[:, t, ns], h_lo[:, t, ns]),
                                 t == 0, t == CT - 1)
                mm.then_inc(split_mm, 1)

            def v_tile(m):
                o = bank(v_use(m))
                ms = slice(m * P, (m + 1) * P)
                for t in range(CT):
                    mm = product(o, (h_hi[:, t, ms], h_lo[:, t, ms]), (pv_hi[:, t, :], pv_lo[:, t, :]),
                                 t == 0, t == CT - 1)
                mm.then_inc(split_mm, 1)

            def scores(chunk, m):
                if m == 0:
                    pe.wait_ge(split_lo, at(b, SPLITS, SPLIT_USES.index((G0, G1)[chunk] + CT - 1) + 1))
                o = bank((S0, S1)[chunk] + m)
                ms = slice(m * P, (m + 1) * P)
                for t in range(CT):
                    mm = product(o, (h_hi[:, t, ms], h_lo[:, t, ms]), (g_hi[:, t, :], g_lo[:, t, :]),
                                 t == 0, t == CT - 1)
                mm.then_inc(raw_mm, 1)

            def outputs(chunk):
                for m in range(NT):
                    pe.wait_ge(pt_lod, at(b, RAWS, chunk * NT + m + 1))
                    for j in range(CT):
                        use = (O0, O1)[chunk] + j
                        o = bank(use) if m == 0 else use % BANKS
                        js = slice(j * P, (j + 1) * P)
                        mm = product(o, (v_hi[:, m, js], v_lo[:, m, js]), (pt_hi[:, m, :], pt_lo[:, m, :]),
                                     m == 0, m == NT - 1)
                    mm.then_inc(out_mm, 1)

            def outputs_by_tile():
                pe.wait_ge(pt_lod, at(b, RAWS, RAWS))
                for j in range(CT):
                    o = bank(O1 + j)
                    js = slice(j * P, (j + 1) * P)
                    for m in range(NT):
                        mm = product(o, (v_hi[:, m, js], v_lo[:, m, js]), (pt_hi[:, m, :], pt_lo[:, m, :]),
                                     m == 0, m == NT - 1)
                    mm.then_inc(out_mm, NT // CT)

            first = isinstance(b, int) and b == 0
            pe.wait_ge(h_lod, at(b, CT, CT))
            for j in range(CT):
                if first and j == 0:
                    pe.wait_ge(vec_out, 2)
                g_tile(0, j)
            if first:
                pe.wait_ge(wp_lod, 2 * CT)
            v_tile(0)
            for m in range(NT):
                scores(0, m)
            for m in range(1, NT - 1):
                v_tile(m)
            for j in range(CT):
                g_tile(1, j)
            v_tile(NT - 1)
            for m in range(NT):
                if nxt is not None and m == NT - 4:
                    pe.wait_ge(split_lo, at(b, SPLITS, SPLIT_USES.index(S1 + NT - 1 - BANKS) + 1))
                    group_mean_mm(pe, nxt, STAT_BANK)
                if nxt is not None and m == NT - 2:
                    group_var_mm(pe, nxt, STAT_BANK)
                if nxt is not None and m == NT - 1:
                    pe.wait_ge(stat, at(nxt, STATS, STATS - 1))
                scores(1, m)
            outputs(0)
            if nxt is not None:
                outputs(1)
            else:
                outputs_by_tile()

        def act_batch(act, b, nxt):
            def g_hi_half(chunk, j):
                use = (G0, G1)[chunk] + j
                act.wait_ge(split_mm, at(b, SPLITS, SPLIT_USES.index(use) + 1))
                nc.scalar.activation(g_hi[:, j, :], ps[:, use % BANKS, :], ACT.Identity,
                                     bias=gbias[:, j:j + 1]).then_inc(split_hi, 1)

            def v_hi_half(m):
                use = v_use(m)
                act.wait_ge(split_mm, at(b, SPLITS, SPLIT_USES.index(use) + 1))
                nc.scalar.activation(v_hi[:, m, :], ps[:, use % BANKS, :], ACT.Copy).then_inc(split_hi, 1)

            def raw_scores(chunk, m):
                k = chunk * NT + m
                act.wait_ge(raw_mm, at(b, RAWS, k + 1))
                wait(act, pt_lod, at(b, RAWS, k + 1 - NT))
                wait(act, summed, at(b, MAXES, (chunk - 1) * (NT - 1) + max(m, 1)))
                nc.scalar.activation(st[:, m, :], ps[:, RAW_USES[k] % BANKS, :], ACT.Copy).then_inc(raw_out, 1)

            def exponentials(chunk, m):
                act.wait_ge(shifted, at(b, RAWS, chunk * NT + m + 1))
                nc.scalar.activation(st[:, m, :], st[:, m, :], ACT.Exp, scale=SCALE).then_inc(exped, 1)

            def pt_hi_half(chunk, m):
                k = chunk * NT + m
                act.wait_ge(exped, at(b, RAWS, k + 1))
                wait(act, out_mm, at(b, RAWS, k + 1 - NT))
                nc.scalar.activation(pt_hi[:, m, :], st[:, m, :], ACT.Copy).then_inc(pt_hid, 1)

            if isinstance(b, int) and b == 0:
                act.wait_ge(vec_out, 1)
            for j in range(CT):
                g_hi_half(0, j)
            v_hi_half(0)
            for m in range(NT):
                raw_scores(0, m)
            v_hi_half(1)
            v_hi_half(2)
            for m in range(NT):
                exponentials(0, m)
                pt_hi_half(0, m)
                if m < NT - 4:
                    v_hi_half(m + 3)
                else:
                    g_hi_half(1, m - (NT - 4))
            v_hi_half(NT - 1)
            for m in range(NT):
                raw_scores(1, m)
            if nxt is not None:
                normalize(act, nxt, 0)
            for m in range(NT):
                exponentials(1, m)
                pt_hi_half(1, m)
                if nxt is not None and m in (1, 3, 5):
                    normalize(act, nxt, (m + 1) // 2)

        def dve_batch(dve, b, nxt):
            def g_lo_half(chunk, j):
                use = (G0, G1)[chunk] + j
                dve.wait_ge(split_hi, at(b, SPLITS, SPLIT_USES.index(use) + 1))
                nc.vector.scalar_tensor_tensor(out=g_lo[:, j, :], in0=ps[:, use % BANKS, :],
                                               scalar=gbias[:, j:j + 1], in1=g_hi[:, j, :].bitcast(F32),
                                               op0=ALU.add, op1=ALU.subtract).then_inc(split_lo, 1)

            def v_lo_half(m):
                use = v_use(m)
                dve.wait_ge(split_hi, at(b, SPLITS, SPLIT_USES.index(use) + 1))
                nc.vector.tensor_tensor(v_lo[:, m, :], ps[:, use % BANKS, :], v_hi[:, m, :].bitcast(F32),
                                        ALU.subtract).then_inc(split_lo, 1)

            def running_max(chunk, m):
                k = chunk * (NT - 1) + m
                dve.wait_ge(raw_out, at(b, RAWS, chunk * NT + m + 1))
                if m == 1:
                    wait(dve, max_all, at(b, 2, chunk))
                else:
                    dve.wait_ge(maxed, at(b, MAXES, k - 1))
                nc.vector.tensor_tensor(rmax[:, :], st[:, 0, :] if m == 1 else rmax[:, :], st[:, m, :],
                                        ALU.max).then_inc(maxed, 1)

            def shift(chunk, m):
                dve.wait_ge(max_all, at(b, 2, chunk + 1))
                nc.vector.tensor_tensor(st[:, m, :], st[:, m, :], cmax[:, :], ALU.subtract).then_inc(shifted, 1)

            def pt_lo_half(chunk, m):
                dve.wait_ge(pt_hid, at(b, RAWS, chunk * NT + m + 1))
                nc.vector.tensor_tensor(pt_lo[:, m, :], st[:, m, :], pt_hi[:, m, :].bitcast(F32),
                                        ALU.subtract).then_inc(pt_lod, 1)

            def finish(chunk):
                dve.wait_ge(sum_all, at(b, 2, chunk + 1))
                nc.vector.reciprocal(rinv[:, chunk, :], rinv[:, chunk, :]).then_inc(inverse, 1)
                dve.wait_ge(inverse, at(b, 2, chunk + 1))
                for j in range(CT):
                    o = ((O0, O1)[chunk] + j) % BANKS
                    dve.wait_ge(out_mm, at(b, RAWS, (chunk + 1) * NT))
                    nc.vector.tensor_tensor(ps[:, o, :], ps[:, o, :], rinv[:, chunk, :], ALU.mult).then_inc(scaled, 1)
                for j in range(CT):
                    o = ((O0, O1)[chunk] + j) % BANKS
                    dve.wait_ge(res_in[chunk], at(b, 16, 16))
                    dve.wait_ge(scaled, at(b, OUTS, chunk * CT + j + 1))
                    nc.vector.scalar_tensor_tensor(out=res[:, chunk, j, :], in0=ps[:, o, :],
                                                   scalar=obias[:, j:j + 1], in1=res[:, chunk, j, :],
                                                   op0=ALU.add, op1=ALU.add).then_inc(finished, 1)

            def finish_by_tile():
                dve.wait_ge(sum_all, at(b, 2, 2))
                nc.vector.reciprocal(rinv[:, 1, :], rinv[:, 1, :]).then_inc(inverse, 1)
                dve.wait_ge(res_in[1], at(b, 16, 16))
                dve.wait_ge(inverse, at(b, 2, 2))
                for j in range(CT):
                    o = (O1 + j) % BANKS
                    dve.wait_ge(out_mm, at(b, RAWS, NT + (j + 1) * NT // CT))
                    nc.vector.tensor_tensor(ps[:, o, :], ps[:, o, :], rinv[:, 1, :], ALU.mult).then_inc(scaled, 1)
                    dve.wait_ge(scaled, at(b, OUTS, CT + j + 1))
                    nc.vector.scalar_tensor_tensor(out=res[:, 1, j, :], in0=ps[:, o, :],
                                                   scalar=obias[:, j:j + 1], in1=res[:, 1, j, :],
                                                   op0=ALU.add, op1=ALU.add).then_inc(finished, 1)

            for j in range(CT):
                g_lo_half(0, j)
            v_lo_half(0)
            for m in range(NT):
                if m:
                    running_max(0, m)
                if nxt is not None:
                    channel_stats(dve, nxt, m)
            if nxt is not None:
                channel_means(dve, nxt)
            v_lo_half(1)
            v_lo_half(2)
            shift(0, 0)
            for m in range(NT):
                if m < NT - 1:
                    shift(0, m + 1)
                pt_lo_half(0, m)
                if m < NT - 4:
                    v_lo_half(m + 3)
                else:
                    g_lo_half(1, m - (NT - 4))
            v_lo_half(NT - 1)
            for m in range(1, NT):
                running_max(1, m)
                if nxt is not None and m == NT - 5:
                    group_deviation(dve, nxt, STAT_BANK)
                if nxt is not None and m == NT - 3:
                    rsqrt_seed(dve, nxt, STAT_BANK)
            shift(1, 0)
            for m in range(NT):
                if m < NT - 1:
                    shift(1, m + 1)
                pt_lo_half(1, m)
                if nxt is not None and m in (1, 3, 5, 7):
                    normalize_lo(dve, nxt, m // 2)
            finish(0)
            if nxt is not None:
                finish(1)
            else:
                finish_by_tile()

        def pool_batch(pool, b, nxt):
            def max_over_partitions(chunk):
                pool.wait_ge(maxed, at(b, MAXES, (chunk + 1) * (NT - 1)))
                wait(pool, shifted, at(b, RAWS, chunk * NT))
                pool.sem_inc(pool_at, 1)
                nc.gpsimd.partition_all_reduce(cmax[:, :], rmax[:, :], P, RMAX).then_inc(max_all, 1)

            def running_sum(chunk, m):
                k = chunk * (NT - 1) + m
                pool.wait_ge(exped, at(b, RAWS, chunk * NT + m + 1))
                if m == 1:
                    wait(pool, sum_all, at(b, 2, chunk))
                else:
                    pool.wait_ge(summed, at(b, MAXES, k - 1))
                nc.gpsimd.tensor_tensor(esum[:, :], st[:, 0, :] if m == 1 else esum[:, :], st[:, m, :],
                                        ALU.add).then_inc(summed, 1)

            def sum_over_partitions(chunk):
                wait(pool, finished, at(b, OUTS, (chunk + 1) * CT - OUTS))
                pool.wait_ge(summed, at(b, MAXES, (chunk + 1) * (NT - 1)))
                pool.sem_inc(pool_at, 1)
                nc.gpsimd.partition_all_reduce(rinv[:, chunk, :], esum[:, :], P, RADD).then_inc(sum_all, 1)

            max_over_partitions(0)
            for m in range(1, NT):
                running_sum(0, m)
            sum_over_partitions(0)
            if nxt is not None:
                norm_coefs(pool, nxt)
            max_over_partitions(1)
            for m in range(1, NT):
                running_sum(1, m)
            sum_over_partitions(1)

        def chunk_of(view, b, ch):
            ns = slice(ch * CH, (ch + 1) * CH)
            if isinstance(b, int):
                return view[b, :, :, ns]
            return view[bass.ds(b, 1), :, :, ns].rearrange("b p j n -> (b p) j n")

        def sp_batch(sp, b, nxt, after):
            for ch in range(2):
                if nxt is None and ch == 1:
                    for j in range(CT):
                        sp.wait_ge(finished, at(b, OUTS, CT + j + 1))
                        sp.dma_start(ov[b, :, j, CH:N], res[:, 1, j, :]).then_inc(stored[1], 16)
                    break
                sp.wait_ge(finished, at(b, OUTS, (ch + 1) * CT))
                sp.dma_start(chunk_of(ov, b, ch), res[:, ch, :, :]).then_inc(stored[ch], 16)
                if nxt is not None:
                    sp.wait_ge(stored[ch], at(b, 16, 16))
                    sp.dma_start(res[:, ch, :, :], chunk_of(xv, nxt, ch)).then_inc(res_in[ch], 16)
                if ch == 0 and after is not None:
                    sp.wait_ge(h_lod, at(nxt, CT, CT))
                    src = xv[after] if isinstance(after, int) else \
                        xv[bass.ds(after, 1), :, :, :].rearrange("b p j n -> (b p) j n")
                    sp.dma_start(xs[:, :, :], src).then_inc(x_in, 16)

        block = ctx.enter_context(nc.Block())

        def batches(eng, body):
            body(eng, 0, 1)
            with eng.Fori(1, B - 1) as b:
                body(eng, b, b + 1)
            body(eng, B - 1, None)

        @block.sync
        def _(sp):
            sp_setup(sp)
            sp_batch(sp, 0, 1, 2)
            with sp.Fori(1, B - 2) as b:
                sp_batch(sp, b, b + 1, b + 2)
            sp_batch(sp, B - 2, B - 1, None)
            sp_batch(sp, B - 1, None, None)
            sp.wait_ge(stored[0], B * 16)
            sp.wait_ge(stored[1], (B - 1 + CT) * 16)

        @block.gpsimd
        def _(pool):
            pool_setup(pool)
            batches(pool, pool_batch)

        @block.tensor
        def _(pe):
            pe_setup(pe)
            batches(pe, pe_batch)

        @block.scalar
        def _(act):
            act_setup(act)
            batches(act, act_batch)

        @block.vector
        def _(dve):
            dve_setup(dve)
            batches(dve, dve_batch)


def kernel(x, L0_conv_gn_w, L0_conv_gn_b, L0_conv_qkv_w, L0_conv_qkv_b, L0_conv_proj_w, L0_conv_proj_b):
    import numpy as np
    import concourse.bacc as bacc
    from concourse.bass_utils import run_bass_kernel_spmd

    def columns(v):
        return np.asarray(v).reshape(-1, P).T

    nc = bacc.Bacc("TRN2", target_bir_lowering=False, num_devices=1)
    host = {
        "x": x, "gn_w": columns(L0_conv_gn_w), "gn_b": columns(L0_conv_gn_b), "qkv_w": L0_conv_qkv_w,
        "qkv_b": columns(L0_conv_qkv_b), "projT": np.asarray(L0_conv_proj_w).T, "proj_b": columns(L0_conv_proj_b),
    }
    arrays = {f"in_{k}": np.ascontiguousarray(a) for k, a in host.items()}
    args = [nc.dram_tensor(k, a.shape, mybir.dt.from_np(a.dtype), kind="ExternalInput").ap()
            for k, a in arrays.items()]
    out = nc.dram_tensor("out", arrays["in_x"].shape, mybir.dt.float32, kind="ExternalOutput").ap()
    group_norm_attention(nc, *args, out)
    r = run_bass_kernel_spmd(nc, [arrays], core_ids=[0])
    return r.results[0]["out"]
```
